# Optimizing a Trainium2 kernel written in Bass

```python
import numpy as np
import jax
import jax.numpy as jnp

def _softmax(x, axis=-1):
    return jax.nn.softmax(x, axis=axis)

def _gelu(x):
    return jax.nn.gelu(x, approximate=True)

def _silu(x):
    return jax.nn.silu(x)

def _sigmoid(x):
    return jax.nn.sigmoid(x)

def _layernorm(x, axis=-1, eps=1e-05):
    m = jnp.mean(x, axis=axis, keepdims=True)
    v = jnp.var(x, axis=axis, keepdims=True)
    return (x - m) / jnp.sqrt(v + eps)

def _scatter_add(tgt, idx, src, axis=0):
    return tgt.at[idx].add(src)

def _segment_sum(src, seg, n):
    return jax.ops.segment_sum(src, seg, n)
kernel_name = 'mk_adaln_d2_jaxref_r8_2cc54f'

def setup_inputs(seed: int=0):
    np.random.seed(seed)
    _w = jnp.asarray

    def _L0_attn_setup():
        import jax, jax.numpy as jnp
        import numpy as np
        EPS = 1e-08

        def polar_orth(W):
            u, s, vt = jnp.linalg.svd(W.astype(jnp.float32), full_matrices=False)
            return u @ vt

        def rms(z):
            return z * jax.lax.rsqrt(jnp.mean(z * z, axis=-1, keepdims=True) + EPS)

        def _reference_tuple_inner(x, Wq, Wv, Wc, Wp1, Wp2, identity):
            B, T, D = x.shape
            P1 = polar_orth(Wp1).astype(x.dtype)
            P2 = polar_orth(Wp2).astype(x.dtype)
            q = jnp.einsum('btd,ed->bte', x, Wq)
            v = jnp.einsum('btd,ed->bte', x, Wv)

            def combine(left, right):
                z = left @ P1.T + right @ P2.T
                return rms(z)
            seq = jnp.concatenate([jnp.broadcast_to(identity.astype(x.dtype), (B, 1, D)), q], axis=1)
            h = jax.lax.associative_scan(combine, seq, axis=1)
            qs = h[:, 1:]
            Y = jnp.einsum('btd,ed->bte', qs * v, Wc)
            return (Y, qs)
        key = jax.random.key(seed)
        ks = jax.random.split(key, 7)
        B, T, D = (4, 512, 128)
        scale = 1.0 / np.sqrt(D)
        x = jax.random.normal(ks[0], (B, T, D), jnp.float32)
        Wq = jax.random.normal(ks[1], (D, D), jnp.float32) * scale
        Wv = jax.random.normal(ks[2], (D, D), jnp.float32) * scale
        Wc = jax.random.normal(ks[3], (D, D), jnp.float32) * scale
        Wp1 = jax.random.normal(ks[4], (D, D), jnp.float32) * scale
        Wp2 = jax.random.normal(ks[5], (D, D), jnp.float32) * scale
        identity = jax.random.uniform(ks[6], (D,), jnp.float32)
        return {'x': x, 'Wq': Wq, 'Wv': Wv, 'Wc': Wc, 'Wp1': Wp1, 'Wp2': Wp2, 'identity': identity}
    _L0_attn_in = _L0_attn_setup()

    def _L0_ffn_setup():
        import jax, jax.numpy as jnp
        import numpy as np
        DIM = 128
        DEPTH = 6
        HEADS = 16
        DIM_HEAD = 64
        WINDOW = 32
        INNER = HEADS * DIM_HEAD
        DIM_INNER = int(DIM * 4 * 2 / 3)
        QK_SCALE = 8.0

        def shift_tokens(t):
            a, s = jnp.split(t, 2, -1)
            s = jnp.pad(s, ((0, 0), (1, 0), (0, 0)))[:, :-1]
            return jnp.concatenate([a, s], -1)

        def l2norm(t):
            return t / jnp.maximum(jnp.linalg.norm(t, axis=-1, keepdims=True), 1e-12)

        def rotate_half(x):
            x1, x2 = jnp.split(x, 2, -1)
            return jnp.concatenate([-x2, x1], -1)

        def rotary_tables(n):
            half = jnp.arange(0, DIM_HEAD, 2, dtype=jnp.float32)
            inv_freq = 1.0 / 10000.0 ** (half / DIM_HEAD)
            t = jnp.arange(n, dtype=jnp.float32)
            freqs = t[:, None] * inv_freq[None, :]
            freqs = jnp.concatenate([freqs, freqs], -1)
            base_scale = (half + 0.4 * DIM_HEAD) / (1.4 * DIM_HEAD)
            power = (t - n // 2) / (WINDOW // 2)
            scale = base_scale[None, :] ** power[:, None]
            scale = jnp.concatenate([scale, scale], -1)
            return (freqs, scale)

        def local_attention(q, k, v):
            b, h, n, d = q.shape
            w = WINDOW
            nw = n // w
            bq = q.reshape(b, h, nw, w, d)
            bk = k.reshape(b, h, nw, w, d)
            bv = v.reshape(b, h, nw, w, d)

            def look(t):
                p = jnp.pad(t, ((0, 0), (0, 0), (1, 0), (0, 0), (0, 0)))
                return jnp.concatenate([p[:, :, :nw], p[:, :, 1:]], axis=3)
            bk2, bv2 = (look(bk), look(bv))
            seq = jnp.arange(n).reshape(nw, w)
            seq_p = jnp.pad(seq, ((1, 0), (0, 0)), constant_values=-1)
            jt = jnp.concatenate([seq_p[:nw], seq_p[1:]], axis=1)
            it = seq[:, :, None]
            jb = jt[:, None, :]
            mask = (it < jb) | (it > jb + w) | (jb == -1)
            sim = jnp.einsum('bhwie,bhwje->bhwij', bq, bk2) * QK_SCALE
            sim = jnp.where(mask, -jnp.finfo(sim.dtype).max, sim)
            attn = jax.nn.softmax(sim, -1)
            out = jnp.einsum('bhwij,bhwje->bhwie', attn, bv2)
            return out.reshape(b, h, n, d)

        def attn_layer(x, Wqkv, qs, ksc, Wo):
            b, n, _ = x.shape
            qkv = x @ Wqkv
            q, k, v = jnp.split(qkv, 3, -1)
            sh = lambda t: t.reshape(b, n, HEADS, DIM_HEAD).transpose(0, 2, 1, 3)
            q, k, v = (sh(q), sh(k), sh(v))
            q = l2norm(q) * qs
            k = l2norm(k) * ksc
            freqs, scale = rotary_tables(n)
            cos, sin = (jnp.cos(freqs), jnp.sin(freqs))
            q = q * cos * scale + rotate_half(q) * sin * scale
            inv = 1.0 / scale
            k = k * cos * inv + rotate_half(k) * sin * inv
            out = local_attention(q, k, v)
            out = out.transpose(0, 2, 1, 3).reshape(b, n, INNER)
            return out @ Wo

        def ffn_layer(x, g, bln, W1, b1, W2, b2):
            mu = x.mean(-1, keepdims=True)
            var = ((x - mu) ** 2).mean(-1, keepdims=True)
            xn = (x - mu) / jnp.sqrt(var + 1e-05) * g + bln
            hg = xn @ W1 + b1
            a, gate = jnp.split(hg, 2, -1)
            return a * jax.nn.gelu(gate, approximate=False) @ W2 + b2
        key = jax.random.key(seed)
        ks = jax.random.split(key, 8)
        B, N = (2, 256)
        init = lambda k, shape: jax.random.normal(k, shape, jnp.float32) * 0.02
        return {'x': jax.random.normal(ks[0], (B, N, DIM), jnp.float32), 'Wqkv': init(ks[1], (DEPTH, DIM, 3 * INNER)), 'q_scale': jnp.ones((DEPTH, DIM_HEAD), jnp.float32), 'k_scale': jnp.ones((DEPTH, DIM_HEAD), jnp.float32), 'Wo': init(ks[2], (DEPTH, INNER, DIM)), 'ln_g': jnp.ones((DEPTH, DIM), jnp.float32), 'ln_b': jnp.zeros((DEPTH, DIM), jnp.float32), 'W1': init(ks[3], (DEPTH, DIM, 2 * DIM_INNER)), 'b1': jnp.zeros((DEPTH, 2 * DIM_INNER), jnp.float32), 'W2': init(ks[4], (DEPTH, DIM_INNER, DIM)), 'b2': jnp.zeros((DEPTH, DIM), jnp.float32)}
    _L0_ffn_in = _L0_ffn_setup()
    _L0_c = _w((lambda *s: np.random.randn(*s).astype(np.float32) * 0.05)(16, 128))
    _L0_wmod = _w((lambda *s: np.random.randn(*s).astype(np.float32) * 0.05)(128, 6 * 128) * 128 ** (-0.5))

    def _L1_attn_setup():
        import jax, jax.numpy as jnp
        import numpy as np
        from jax import lax
        B, L = (2, 256)
        DIM, HEADS = (128, 16)
        HD = DIM // HEADS
        D_STATE, D_CONV = (16, 4)
        D_INNER = 2 * DIM
        DT_RANK = DIM // 16

        def _mqa(x, wqkv, bqkv, w_attn_out, b_attn_out):
            b, l, d = x.shape
            qkv = x @ wqkv + bqkv
            q = qkv[..., :DIM].reshape(b, l, HEADS, HD)
            k = qkv[..., DIM:DIM + HD]
            v = qkv[..., DIM + HD:]
            scores = jnp.einsum('blhd,bmd->bhlm', q, k) / np.sqrt(HD).astype(np.float32)
            causal = jnp.tril(jnp.ones((l, l), bool))
            scores = jnp.where(causal, scores, jnp.finfo(scores.dtype).min)
            attn = jax.nn.softmax(scores, axis=-1)
            out = jnp.einsum('bhlm,bmd->blhd', attn, v).reshape(b, l, DIM)
            return out @ w_attn_out + b_attn_out

        def _mamba(x, w_in, conv_w, conv_b, w_xproj, w_dt, b_dt, A_log, Dp, w_out):
            b, l, d = x.shape
            xr = x @ w_in
            u0, res = (xr[..., :D_INNER], xr[..., D_INNER:])
            lhs = u0.transpose(0, 2, 1)
            rhs = conv_w[:, None, :]
            xc = lax.conv_general_dilated(lhs, rhs, window_strides=(1,), padding=[(D_CONV - 1, 0)], dimension_numbers=('NCH', 'OIH', 'NCH'), feature_group_count=D_INNER)
            u = jax.nn.silu((xc + conv_b[None, :, None]).transpose(0, 2, 1))
            x_dbl = u @ w_xproj
            delta = jax.nn.softplus(x_dbl[..., :DT_RANK] @ w_dt + b_dt)
            Bm = x_dbl[..., DT_RANK:DT_RANK + D_STATE]
            Cm = x_dbl[..., DT_RANK + D_STATE:]
            A = -jnp.exp(A_log)

            def step(h, inp):
                d_t, b_t, c_t, u_t = inp
                dA = jnp.exp(d_t[..., None] * A)
                h = dA * h + (d_t * u_t)[..., None] * b_t[:, None, :]
                y = jnp.einsum('bdn,bn->bd', h, c_t)
                return (h, y)
            xs = (delta.transpose(1, 0, 2), Bm.transpose(1, 0, 2), Cm.transpose(1, 0, 2), u.transpose(1, 0, 2))
            h0 = jnp.zeros((b, D_INNER, D_STATE), u.dtype)
            _, ys = lax.scan(step, h0, xs)
            y = ys.transpose(1, 0, 2) + u * Dp
            y = y * jax.nn.silu(res)
            return y @ w_out
        key = jax.random.key(seed)
        ks = jax.random.split(key, 12)
        w = lambda k, shape, s=0.02: jax.random.normal(k, shape, jnp.float32) * s
        A_log = jnp.log(jnp.tile(jnp.arange(1, D_STATE + 1, dtype=jnp.float32), (D_INNER, 1)))
        return {'x': jax.random.normal(ks[0], (B, L, DIM), jnp.float32), 'wqkv': w(ks[1], (DIM, DIM + 2 * HD)), 'bqkv': jnp.zeros((DIM + 2 * HD,), jnp.float32), 'w_attn_out': w(ks[2], (DIM, DIM)), 'b_attn_out': jnp.zeros((DIM,), jnp.float32), 'w_in': w(ks[3], (DIM, 2 * D_INNER)), 'conv_w': w(ks[4], (D_INNER, D_CONV), 0.1), 'conv_b': jnp.zeros((D_INNER,), jnp.float32), 'w_xproj': w(ks[5], (D_INNER, DT_RANK + 2 * D_STATE)), 'w_dt': w(ks[6], (DT_RANK, D_INNER)), 'b_dt': w(ks[7], (D_INNER,), 0.01), 'A_log': A_log, 'Dp': jnp.ones((D_INNER,), jnp.float32), 'w_out': w(ks[8], (D_INNER, DIM))}
    _L1_attn_in = _L1_attn_setup()

    def _L1_ffn_setup():
        import jax, jax.numpy as jnp
        import numpy as np
        HIDDEN = 128
        N_ROUTED = 16
        N_SHARED = 2
        TOP_K = 2
        MID_R = HIDDEN // 4
        MID_S = HIDDEN // 2
        key = jax.random.key(seed)
        ks = jax.random.split(key, 8)
        s = 0.02
        return {'x': jax.random.normal(ks[0], (2, 128, HIDDEN), dtype=jnp.float32), 'router_w': jax.random.normal(ks[1], (HIDDEN, N_ROUTED), dtype=jnp.float32) * s, 'wg_r': jax.random.normal(ks[2], (N_ROUTED, HIDDEN, MID_R), dtype=jnp.float32) * s, 'wu_r': jax.random.normal(ks[3], (N_ROUTED, HIDDEN, MID_R), dtype=jnp.float32) * s, 'wd_r': jax.random.normal(ks[4], (N_ROUTED, MID_R, HIDDEN), dtype=jnp.float32) * s, 'wg_s': jax.random.normal(ks[5], (N_SHARED, HIDDEN, MID_S), dtype=jnp.float32) * s, 'wu_s': jax.random.normal(ks[6], (N_SHARED, HIDDEN, MID_S), dtype=jnp.float32) * s, 'wd_s': jax.random.normal(ks[7], (N_SHARED, MID_S, HIDDEN), dtype=jnp.float32) * s}
    _L1_ffn_in = _L1_ffn_setup()
    _L1_c = _w((lambda *s: np.random.randn(*s).astype(np.float32) * 0.05)(16, 128))
    _L1_wmod = _w((lambda *s: np.random.randn(*s).astype(np.float32) * 0.05)(128, 6 * 128) * 128 ** (-0.5))
    _d = {'L0_attn_x': _L0_attn_in['x'], 'L0_attn_Wq': _L0_attn_in['Wq'], 'L0_attn_Wv': _L0_attn_in['Wv'], 'L0_attn_Wc': _L0_attn_in['Wc'], 'L0_attn_Wp1': _L0_attn_in['Wp1'], 'L0_attn_Wp2': _L0_attn_in['Wp2'], 'L0_attn_identity': _L0_attn_in['identity'], 'L0_ffn_Wqkv': _L0_ffn_in['Wqkv'], 'L0_ffn_q_scale': _L0_ffn_in['q_scale'], 'L0_ffn_k_scale': _L0_ffn_in['k_scale'], 'L0_ffn_Wo': _L0_ffn_in['Wo'], 'L0_ffn_ln_g': _L0_ffn_in['ln_g'], 'L0_ffn_ln_b': _L0_ffn_in['ln_b'], 'L0_ffn_W1': _L0_ffn_in['W1'], 'L0_ffn_b1': _L0_ffn_in['b1'], 'L0_ffn_W2': _L0_ffn_in['W2'], 'L0_ffn_b2': _L0_ffn_in['b2'], 'L0_c': _L0_c, 'L0_wmod': _L0_wmod, 'L1_attn_wqkv': _L1_attn_in['wqkv'], 'L1_attn_bqkv': _L1_attn_in['bqkv'], 'L1_attn_w_attn_out': _L1_attn_in['w_attn_out'], 'L1_attn_b_attn_out': _L1_attn_in['b_attn_out'], 'L1_attn_w_in': _L1_attn_in['w_in'], 'L1_attn_conv_w': _L1_attn_in['conv_w'], 'L1_attn_conv_b': _L1_attn_in['conv_b'], 'L1_attn_w_xproj': _L1_attn_in['w_xproj'], 'L1_attn_w_dt': _L1_attn_in['w_dt'], 'L1_attn_b_dt': _L1_attn_in['b_dt'], 'L1_attn_A_log': _L1_attn_in['A_log'], 'L1_attn_Dp': _L1_attn_in['Dp'], 'L1_attn_w_out': _L1_attn_in['w_out'], 'L1_ffn_router_w': _L1_ffn_in['router_w'], 'L1_ffn_wg_r': _L1_ffn_in['wg_r'], 'L1_ffn_wu_r': _L1_ffn_in['wu_r'], 'L1_ffn_wd_r': _L1_ffn_in['wd_r'], 'L1_ffn_wg_s': _L1_ffn_in['wg_s'], 'L1_ffn_wu_s': _L1_ffn_in['wu_s'], 'L1_ffn_wd_s': _L1_ffn_in['wd_s'], 'L1_c': _L1_c, 'L1_wmod': _L1_wmod}
    _x0 = _d['L0_attn_x']
    _d['L0_attn_x'] = jax.random.normal(jax.random.fold_in(jax.random.key(seed), 1), (16, 256, 128), dtype=_x0.dtype)
    del _x0
    return _d

def reference(L0_attn_x, L0_attn_Wq, L0_attn_Wv, L0_attn_Wc, L0_attn_Wp1, L0_attn_Wp2, L0_attn_identity, L0_ffn_Wqkv, L0_ffn_q_scale, L0_ffn_k_scale, L0_ffn_Wo, L0_ffn_ln_g, L0_ffn_ln_b, L0_ffn_W1, L0_ffn_b1, L0_ffn_W2, L0_ffn_b2, L0_c, L0_wmod, L1_attn_wqkv, L1_attn_bqkv, L1_attn_w_attn_out, L1_attn_b_attn_out, L1_attn_w_in, L1_attn_conv_w, L1_attn_conv_b, L1_attn_w_xproj, L1_attn_w_dt, L1_attn_b_dt, L1_attn_A_log, L1_attn_Dp, L1_attn_w_out, L1_ffn_router_w, L1_ffn_wg_r, L1_ffn_wu_r, L1_ffn_wd_r, L1_ffn_wg_s, L1_ffn_wu_s, L1_ffn_wd_s, L1_c, L1_wmod):

    def _L0_attn_ref(x, Wq, Wv, Wc, Wp1, Wp2, identity):
        import jax, jax.numpy as jnp
        import numpy as np
        EPS = 1e-08

        def polar_orth(W):
            u, s, vt = jnp.linalg.svd(W.astype(jnp.float32), full_matrices=False)
            return u @ vt

        def rms(z):
            return z * jax.lax.rsqrt(jnp.mean(z * z, axis=-1, keepdims=True) + EPS)

        def _reference_tuple_inner(x, Wq, Wv, Wc, Wp1, Wp2, identity):
            B, T, D = x.shape
            P1 = polar_orth(Wp1).astype(x.dtype)
            P2 = polar_orth(Wp2).astype(x.dtype)
            q = jnp.einsum('btd,ed->bte', x, Wq)
            v = jnp.einsum('btd,ed->bte', x, Wv)

            def combine(left, right):
                z = left @ P1.T + right @ P2.T
                return rms(z)
            seq = jnp.concatenate([jnp.broadcast_to(identity.astype(x.dtype), (B, 1, D)), q], axis=1)
            h = jax.lax.associative_scan(combine, seq, axis=1)
            qs = h[:, 1:]
            Y = jnp.einsum('btd,ed->bte', qs * v, Wc)
            return (Y, qs)
        return _reference_tuple_inner(x, Wq, Wv, Wc, Wp1, Wp2, identity)[0]

    def _L0_ffn_ref(x, Wqkv, q_scale, k_scale, Wo, ln_g, ln_b, W1, b1, W2, b2):
        import jax, jax.numpy as jnp
        import numpy as np
        DIM = 128
        DEPTH = 6
        HEADS = 16
        DIM_HEAD = 64
        WINDOW = 32
        INNER = HEADS * DIM_HEAD
        DIM_INNER = int(DIM * 4 * 2 / 3)
        QK_SCALE = 8.0

        def shift_tokens(t):
            a, s = jnp.split(t, 2, -1)
            s = jnp.pad(s, ((0, 0), (1, 0), (0, 0)))[:, :-1]
            return jnp.concatenate([a, s], -1)

        def l2norm(t):
            return t / jnp.maximum(jnp.linalg.norm(t, axis=-1, keepdims=True), 1e-12)

        def rotate_half(x):
            x1, x2 = jnp.split(x, 2, -1)
            return jnp.concatenate([-x2, x1], -1)

        def rotary_tables(n):
            half = jnp.arange(0, DIM_HEAD, 2, dtype=jnp.float32)
            inv_freq = 1.0 / 10000.0 ** (half / DIM_HEAD)
            t = jnp.arange(n, dtype=jnp.float32)
            freqs = t[:, None] * inv_freq[None, :]
            freqs = jnp.concatenate([freqs, freqs], -1)
            base_scale = (half + 0.4 * DIM_HEAD) / (1.4 * DIM_HEAD)
            power = (t - n // 2) / (WINDOW // 2)
            scale = base_scale[None, :] ** power[:, None]
            scale = jnp.concatenate([scale, scale], -1)
            return (freqs, scale)

        def local_attention(q, k, v):
            b, h, n, d = q.shape
            w = WINDOW
            nw = n // w
            bq = q.reshape(b, h, nw, w, d)
            bk = k.reshape(b, h, nw, w, d)
            bv = v.reshape(b, h, nw, w, d)

            def look(t):
                p = jnp.pad(t, ((0, 0), (0, 0), (1, 0), (0, 0), (0, 0)))
                return jnp.concatenate([p[:, :, :nw], p[:, :, 1:]], axis=3)
            bk2, bv2 = (look(bk), look(bv))
            seq = jnp.arange(n).reshape(nw, w)
            seq_p = jnp.pad(seq, ((1, 0), (0, 0)), constant_values=-1)
            jt = jnp.concatenate([seq_p[:nw], seq_p[1:]], axis=1)
            it = seq[:, :, None]
            jb = jt[:, None, :]
            mask = (it < jb) | (it > jb + w) | (jb == -1)
            sim = jnp.einsum('bhwie,bhwje->bhwij', bq, bk2) * QK_SCALE
            sim = jnp.where(mask, -jnp.finfo(sim.dtype).max, sim)
            attn = jax.nn.softmax(sim, -1)
            out = jnp.einsum('bhwij,bhwje->bhwie', attn, bv2)
            return out.reshape(b, h, n, d)

        def attn_layer(x, Wqkv, qs, ksc, Wo):
            b, n, _ = x.shape
            qkv = x @ Wqkv
            q, k, v = jnp.split(qkv, 3, -1)
            sh = lambda t: t.reshape(b, n, HEADS, DIM_HEAD).transpose(0, 2, 1, 3)
            q, k, v = (sh(q), sh(k), sh(v))
            q = l2norm(q) * qs
            k = l2norm(k) * ksc
            freqs, scale = rotary_tables(n)
            cos, sin = (jnp.cos(freqs), jnp.sin(freqs))
            q = q * cos * scale + rotate_half(q) * sin * scale
            inv = 1.0 / scale
            k = k * cos * inv + rotate_half(k) * sin * inv
            out = local_attention(q, k, v)
            out = out.transpose(0, 2, 1, 3).reshape(b, n, INNER)
            return out @ Wo

        def ffn_layer(x, g, bln, W1, b1, W2, b2):
            mu = x.mean(-1, keepdims=True)
            var = ((x - mu) ** 2).mean(-1, keepdims=True)
            xn = (x - mu) / jnp.sqrt(var + 1e-05) * g + bln
            hg = xn @ W1 + b1
            a, gate = jnp.split(hg, 2, -1)
            return a * jax.nn.gelu(gate, approximate=False) @ W2 + b2
        for i in range(DEPTH):
            x = attn_layer(shift_tokens(x), Wqkv[i], q_scale[i], k_scale[i], Wo[i]) + x
            x = ffn_layer(shift_tokens(x), ln_g[i], ln_b[i], W1[i], b1[i], W2[i], b2[i]) + x
        return x

    def _L1_attn_ref(x, wqkv, bqkv, w_attn_out, b_attn_out, w_in, conv_w, conv_b, w_xproj, w_dt, b_dt, A_log, Dp, w_out):
        import jax, jax.numpy as jnp
        import numpy as np
        from jax import lax
        B, L = (2, 256)
        DIM, HEADS = (128, 16)
        HD = DIM // HEADS
        D_STATE, D_CONV = (16, 4)
        D_INNER = 2 * DIM
        DT_RANK = DIM // 16

        def _mqa(x, wqkv, bqkv, w_attn_out, b_attn_out):
            b, l, d = x.shape
            qkv = x @ wqkv + bqkv
            q = qkv[..., :DIM].reshape(b, l, HEADS, HD)
            k = qkv[..., DIM:DIM + HD]
            v = qkv[..., DIM + HD:]
            scores = jnp.einsum('blhd,bmd->bhlm', q, k) / np.sqrt(HD).astype(np.float32)
            causal = jnp.tril(jnp.ones((l, l), bool))
            scores = jnp.where(causal, scores, jnp.finfo(scores.dtype).min)
            attn = jax.nn.softmax(scores, axis=-1)
            out = jnp.einsum('bhlm,bmd->blhd', attn, v).reshape(b, l, DIM)
            return out @ w_attn_out + b_attn_out

        def _mamba(x, w_in, conv_w, conv_b, w_xproj, w_dt, b_dt, A_log, Dp, w_out):
            b, l, d = x.shape
            xr = x @ w_in
            u0, res = (xr[..., :D_INNER], xr[..., D_INNER:])
            lhs = u0.transpose(0, 2, 1)
            rhs = conv_w[:, None, :]
            xc = lax.conv_general_dilated(lhs, rhs, window_strides=(1,), padding=[(D_CONV - 1, 0)], dimension_numbers=('NCH', 'OIH', 'NCH'), feature_group_count=D_INNER)
            u = jax.nn.silu((xc + conv_b[None, :, None]).transpose(0, 2, 1))
            x_dbl = u @ w_xproj
            delta = jax.nn.softplus(x_dbl[..., :DT_RANK] @ w_dt + b_dt)
            Bm = x_dbl[..., DT_RANK:DT_RANK + D_STATE]
            Cm = x_dbl[..., DT_RANK + D_STATE:]
            A = -jnp.exp(A_log)

            def step(h, inp):
                d_t, b_t, c_t, u_t = inp
                dA = jnp.exp(d_t[..., None] * A)
                h = dA * h + (d_t * u_t)[..., None] * b_t[:, None, :]
                y = jnp.einsum('bdn,bn->bd', h, c_t)
                return (h, y)
            xs = (delta.transpose(1, 0, 2), Bm.transpose(1, 0, 2), Cm.transpose(1, 0, 2), u.transpose(1, 0, 2))
            h0 = jnp.zeros((b, D_INNER, D_STATE), u.dtype)
            _, ys = lax.scan(step, h0, xs)
            y = ys.transpose(1, 0, 2) + u * Dp
            y = y * jax.nn.silu(res)
            return y @ w_out
        attended = _mqa(x, wqkv, bqkv, w_attn_out, b_attn_out)
        x1 = attended + x
        y = _mamba(x1, w_in, conv_w, conv_b, w_xproj, w_dt, b_dt, A_log, Dp, w_out)
        return y + x1

    def _L1_ffn_ref(x, router_w, wg_r, wu_r, wd_r, wg_s, wu_s, wd_s):
        import jax, jax.numpy as jnp
        import numpy as np
        HIDDEN = 128
        N_ROUTED = 16
        N_SHARED = 2
        TOP_K = 2
        MID_R = HIDDEN // 4
        MID_S = HIDDEN // 2
        orig_shape = x.shape
        flat = x.reshape(-1, orig_shape[-1])
        gs = jnp.einsum('td,ndm->tnm', flat, wg_s)
        us = jnp.einsum('td,ndm->tnm', flat, wu_s)
        out = jnp.einsum('tnm,nmd->td', jax.nn.silu(gs) * us, wd_s)
        logits = (flat @ router_w).astype(jnp.float32)
        probs = jax.nn.softmax(logits, axis=-1)
        weights, indices = jax.lax.top_k(probs, TOP_K)
        weights = weights / (weights.sum(axis=-1, keepdims=True) + 1e-09)
        weights = weights.astype(x.dtype)
        comb = jnp.sum(jax.nn.one_hot(indices, N_ROUTED, dtype=x.dtype) * weights[..., None], axis=1)
        g = jnp.einsum('td,edm->tem', flat, wg_r)
        u = jnp.einsum('td,edm->tem', flat, wu_r)
        h = jax.nn.silu(g) * u
        h = h * comb[:, :, None]
        out = out + jnp.einsum('tem,emd->td', h, wd_r)
        return out.reshape(orig_shape)
    x = L0_attn_x
    mod = (_silu(L0_c) @ L0_wmod).reshape(L0_c.shape[0], 6, 1, -1)
    sa, ca, ga, sb, cb, gb = (mod[:, 0], mod[:, 1], mod[:, 2], mod[:, 3], mod[:, 4], mod[:, 5])
    ga = (2 * (ga >= 0) - 1) * jnp.maximum(jnp.abs(ga), 0.25)
    gb = (2 * (gb >= 0) - 1) * jnp.maximum(jnp.abs(gb), 0.25)
    h = _layernorm(x, axis=-1) * (1 + ca) + sa
    x = x + ga * _L0_attn_ref(h, L0_attn_Wq, L0_attn_Wv, L0_attn_Wc, L0_attn_Wp1, L0_attn_Wp2, L0_attn_identity)
    h = _layernorm(x, axis=-1) * (1 + cb) + sb
    x = x + gb * _L0_ffn_ref(h, L0_ffn_Wqkv, L0_ffn_q_scale, L0_ffn_k_scale, L0_ffn_Wo, L0_ffn_ln_g, L0_ffn_ln_b, L0_ffn_W1, L0_ffn_b1, L0_ffn_W2, L0_ffn_b2)
    mod = (_silu(L1_c) @ L1_wmod).reshape(L1_c.shape[0], 6, 1, -1)
    sa, ca, ga, sb, cb, gb = (mod[:, 0], mod[:, 1], mod[:, 2], mod[:, 3], mod[:, 4], mod[:, 5])
    ga = (2 * (ga >= 0) - 1) * jnp.maximum(jnp.abs(ga), 0.25)
    gb = (2 * (gb >= 0) - 1) * jnp.maximum(jnp.abs(gb), 0.25)
    h = _layernorm(x, axis=-1) * (1 + ca) + sa
    x = x + ga * _L1_attn_ref(h, L1_attn_wqkv, L1_attn_bqkv, L1_attn_w_attn_out, L1_attn_b_attn_out, L1_attn_w_in, L1_attn_conv_w, L1_attn_conv_b, L1_attn_w_xproj, L1_attn_w_dt, L1_attn_b_dt, L1_attn_A_log, L1_attn_Dp, L1_attn_w_out)
    h = _layernorm(x, axis=-1) * (1 + cb) + sb
    x = x + gb * _L1_ffn_ref(h, L1_ffn_router_w, L1_ffn_wg_r, L1_ffn_wu_r, L1_ffn_wd_r, L1_ffn_wg_s, L1_ffn_wu_s, L1_ffn_wd_s)
    return x

_drawn_inputs = setup_inputs


def setup_inputs(seed=0):
    import zlib

    import numpy as np

    out = dict(_drawn_inputs(seed))
    spreads = {'L0_ffn_q_scale': (1.0, 0.2),
     'L0_ffn_k_scale': (1.0, 0.2),
     'L0_ffn_ln_g': (1.0, 0.2),
     'L0_ffn_ln_b': (0.0, 0.1),
     'L0_ffn_b1': (0.0, 0.1),
     'L0_ffn_b2': (0.0, 0.1),
     'L1_attn_bqkv': (0.0, 0.1),
     'L1_attn_b_attn_out': (0.0, 0.1),
     'L1_attn_conv_b': (0.0, 0.1),
     'L1_attn_Dp': (1.0, 0.2)}
    factors = {}
    for name, (base, spread) in spreads.items():
        noise = np.random.default_rng([zlib.crc32(name.encode()), seed]).standard_normal(out[name].shape)
        drawn = base * np.exp(spread * noise) if base else spread * noise
        out[name] = jnp.asarray(drawn.astype(out[name].dtype))
    for name, factor in factors.items():
        out[name] = (out[name] * factor).astype(out[name].dtype)
    return out
```

```python
from contextlib import ExitStack

import numpy as np

import concourse.bass as bass
from concourse import mybir

ALU = mybir.AluOpType
ACT = mybir.ActivationFunctionType
AX = mybir.AxisListType
F32 = mybir.dt.float32
BF16 = mybir.dt.bfloat16

P = 128
B = 16
T = 256
TT = T // P
NT = B * TT
LN_EPS = 1e-5


class Kernel:

    def __init__(self, nc, dram, out, ctx):
        self.nc, self.dram, self.out, self.ctx = nc, dram, out, ctx

    def sb(self, ctx, name, shape, dt=F32):
        return ctx.enter_context(self.nc.sbuf_tensor(name, shape, dt))

    def ps(self, ctx, name, shape, dt=F32):
        return ctx.enter_context(self.nc.psum_tensor(name, shape, dt))


def sems(nc, ctx, names):
    return [ctx.enter_context(nc.semaphore(n)) for n in names.split()]


def clear_released_semaphores(nc):
    ids = sorted(nc.released_uncleared_semaphores)
    nc.all_engine_barrier()
    first = ids[0]
    for this, after in zip(ids, ids[1:] + [None]):
        if after != this + 1:
            nc.gpsimd.sem_clear(range(first, this + 1))
            first = after
    nc.all_engine_barrier()


def setup_stage(k):
    nc, d = k.nc, k.dram
    with ExitStack() as ctx:
        cT = k.sb(ctx, "cT", [P, 2, B])
        wmod = k.sb(ctx, "wmod", [P, 2, 6 * P])
        sig = k.sb(ctx, "sig", [P, 2, B])
        silu = k.sb(ctx, "silu", [P, 2, B])
        gate_abs = k.sb(ctx, "gate_abs", [P, 4, B])
        gate_sign = k.sb(ctx, "gate_sign", [P, 4, B])
        mod_ps = k.ps(ctx, "mod_ps", [P, 12, B])
        loaded, exped, siluing, silu_ready, mod_ready, gating, gate_ready = sems(
            nc, ctx, "su_loaded su_exped su_siluing su_silu_ready su_mod_ready su_gating su_gate_ready")
        block = ctx.enter_context(nc.Block())

        @block.sync
        def _(sp):
            sp.dma_start(cT[:, :, :], d["cT"]).then_inc(loaded, 16)
            sp.dma_start(wmod[:, 0, :], d["L0_wmod"]).then_inc(loaded, 16)
            sp.dma_start(wmod[:, 1, :], d["L1_wmod"]).then_inc(loaded, 16)
            sp.dma_start(k.ident[:, :], d["ident"]).then_inc(loaded, 16)
            sp.dma_start(k.x[:, :, :], d["L0_attn_x"].rearrange("b (t p) d -> p (b t) d", p=P)).then_inc(loaded, 16)

        @block.scalar
        def _(act):
            act.wait_ge(loaded, 80)
            nc.scalar.activation(sig[:, :, :], cT[:, :, :], ACT.Exp, scale=-1.0).then_inc(exped, 1)

        @block.vector
        def _(dve):
            dve.wait_ge(exped, 1)
            nc.vector.tensor_scalar(sig[:, :, :], sig[:, :, :], 1.0, None, ALU.add).then_inc(siluing, 1)
            dve.wait_ge(siluing, 1)
            nc.vector.reciprocal(sig[:, :, :], sig[:, :, :]).then_inc(siluing, 1)
            dve.wait_ge(siluing, 2)
            nc.vector.tensor_tensor(silu[:, :, :], sig[:, :, :], cT[:, :, :], ALU.mult).then_inc(silu_ready, 1)
            dve.wait_ge(mod_ready, 1)
            for layer in range(2):
                for half in range(2):
                    s, c, g = (6 * layer + 3 * half + i for i in range(3))
                    m = 2 * layer + half
                    nc.vector.tensor_copy(k.shift[:, m, :], mod_ps[:, s, :])
                    nc.vector.tensor_scalar(k.scale1[:, m, :], mod_ps[:, c, :], 1.0, None, ALU.add)
                    nc.vector.tensor_scalar(gate_sign[:, m, :], mod_ps[:, g, :], 0.0, 2.0, ALU.is_ge, ALU.mult)\
                        .then_inc(gating, 1)
                    dve.wait_ge(gating, 4 * m + 1)
                    nc.vector.tensor_scalar(gate_sign[:, m, :], gate_sign[:, m, :], -1.0, None, ALU.add)\
                        .then_inc(gating, 1)
                    dve.wait_ge(gating, 4 * m + 2)
                    nc.vector.tensor_tensor(gate_abs[:, m, :], mod_ps[:, g, :], gate_sign[:, m, :], ALU.mult)\
                        .then_inc(gating, 1)
                    dve.wait_ge(gating, 4 * m + 3)
                    nc.vector.tensor_scalar(gate_abs[:, m, :], gate_abs[:, m, :], 0.25, None, ALU.max)\
                        .then_inc(gating, 1)
                    dve.wait_ge(gating, 4 * m + 4)
                    nc.vector.tensor_tensor(k.gate[:, m, :], gate_abs[:, m, :], gate_sign[:, m, :], ALU.mult)\
                        .then_inc(gate_ready, 1)

        @block.tensor
        def _(pe):
            pe.wait_ge(silu_ready, 1)
            for m in range(12):
                last = nc.tensor.matmul(mod_ps[:, m, :], wmod[:, m // 6, (m % 6) * P:(m % 6 + 1) * P],
                                        silu[:, m // 6, :], start=True, stop=True)
            last.then_inc(mod_ready, 1)


def polar_schedule(low=1e-6):
    steps = []
    while low < 1 - 1e-7:
        r = 1.0 / (1 + low + low * low)
        a = 1.5 * (3 * r) ** 0.5
        b = a * r
        margin = 1.01 if low < 0.3 else 1.0
        a, b = a / margin, b / margin ** 3
        low = low * (a - b * low * low)
        steps.append((a, b))
    return steps + [(1.5, 0.5)] * 2


def polar_stage(k):
    nc, d = k.nc, k.dram
    steps = polar_schedule()
    with ExitStack() as ctx:
        X = k.sb(ctx, "polar_X", [P, 2, P])
        M = k.sb(ctx, "polar_M", [P, 2, P])
        sq = k.sb(ctx, "polar_sq", [P, 2, P])
        rows = k.sb(ctx, "polar_rows", [P, 2])
        norm = k.sb(ctx, "polar_norm", [P, 2])
        ones = k.sb(ctx, "polar_ones", [P, P])
        G = k.ps(ctx, "polar_G", [P, 512])
        XN = k.ps(ctx, "polar_XN", [P, 512])
        TN = k.ps(ctx, "polar_TN", [P, 512])
        NN = k.ps(ctx, "polar_NN", [P, 2])
        loaded, squared, rowed, summed, normed, scaled, gram, poly, next_x, next_t, stored = sems(
            nc, ctx, "po_loaded po_squared po_rowed po_summed po_normed po_scaled po_gram po_poly po_next_x po_next_t po_stored")
        block = ctx.enter_context(nc.Block())
        v = lambda t: t[:, 0:2 * P].rearrange("p (i c) -> p i c", i=2)

        @block.sync
        def _(sp):
            for i in range(2):
                sp.dma_start(X[:, i, :], d[f"L0_attn_Wp{i + 1}"]).then_inc(loaded, 16)
                sp.dma_start(k.PT[:, i, :], d[f"Wp{i + 1}T"]).then_inc(loaded, 16)

        @block.scalar
        def _(act):
            act.wait_ge(summed, 1)
            nc.scalar.activation(norm[:, :], NN[:, :], ACT.Sqrt).then_inc(normed, 1)
            for n in range(len(steps)):
                act.wait_ge(next_x, n + 1)
                nc.scalar.activation(X[:, :, :], v(XN), ACT.Copy).then_inc(stored, 1)

        @block.vector
        def _(dve):
            nc.vector.memset(ones[:, :], 1.0).then_inc(squared, 1)
            dve.wait_ge(loaded, 64)
            nc.vector.tensor_tensor(sq[:, :, :], X[:, :, :], X[:, :, :], ALU.mult).then_inc(squared, 1)
            dve.wait_ge(squared, 2)
            nc.vector.tensor_reduce(rows[:, :], sq[:, :, :], AX.X, ALU.add).then_inc(rowed, 1)
            dve.wait_ge(normed, 1)
            nc.vector.reciprocal(norm[:, :], norm[:, :]).then_inc(normed, 1)
            dve.wait_ge(normed, 2)
            for i in range(2):
                nc.vector.tensor_scalar(X[:, i, :], X[:, i, :], norm[:, i:i + 1], None, ALU.mult)
                last = nc.vector.tensor_scalar(k.PT[:, i, :], k.PT[:, i, :], norm[:, i:i + 1], None, ALU.mult)
            last.then_inc(scaled, 1)
            for n, (a, b) in enumerate(steps):
                dve.wait_ge(gram, n + 1)
                if n:
                    dve.wait_ge(next_t, n)
                nc.vector.tensor_scalar(M[:, :, :], v(G), -b, None, ALU.mult).then_inc(poly, 1)
                dve.wait_ge(poly, 2 * n + 1)
                for i in range(2):
                    last = nc.vector.scalar_tensor_tensor(out=M[:, i, :], in0=k.ident[:, :], scalar=a, in1=M[:, i, :],
                                                          op0=ALU.mult, op1=ALU.add)
                last.then_inc(poly, 1)
                dve.wait_ge(next_t, n + 1)
                nc.vector.tensor_copy(k.PT[:, :, :], v(TN)).then_inc(scaled, 1)

        @block.tensor
        def _(pe):
            pe.wait_ge(rowed, 1)
            nc.tensor.matmul(NN[:, :], ones[:, :], rows[:, :], start=True, stop=True).then_inc(summed, 1)
            for n in range(len(steps)):
                pe.wait_ge(scaled, n + 1)
                if n:
                    pe.wait_ge(stored, n)
                for i in range(2):
                    last = nc.tensor.matmul(v(G)[:, i, :], X[:, i, :], X[:, i, :], start=True, stop=True)
                last.then_inc(gram, 1)
                pe.wait_ge(poly, 2 * n + 2)
                for i in range(2):
                    last = nc.tensor.matmul(v(XN)[:, i, :], k.PT[:, i, :], M[:, i, :], start=True, stop=True)
                last.then_inc(next_x, 1)
                for i in range(2):
                    last = nc.tensor.matmul(v(TN)[:, i, :], M[:, i, :], k.PT[:, i, :], start=True, stop=True)
                last.then_inc(next_t, 1)


def rows_stage(k, which, pairs):
    nc = k.nc
    with ExitStack() as ctx:
        row_ps = k.ps(ctx, f"rows{which}_ps", [P, 2, 4, P])
        filled, copied = sems(nc, ctx, f"ro{which}_filled ro{which}_copied")
        block = ctx.enter_context(nc.Block())
        fills = [(source, target, c) for source, target in pairs for c in range(0, B, 4)]

        @block.tensor
        def _(pe):
            for f, (source, target, c) in enumerate(fills):
                if f >= 2:
                    pe.wait_ge(copied, f - 1)
                for i in range(4):
                    last = nc.tensor.matmul(row_ps[:, f % 2, i, :], source[:, c + i:c + i + 1].to_broadcast([P, P]),
                                            k.ident[:, :], start=True, stop=True)
                last.then_inc(filled, 1)

        @block.vector
        def _(dve):
            for f, (source, target, c) in enumerate(fills):
                dve.wait_ge(filled, f + 1)
                nc.vector.tensor_copy(target[:, c:c + 4, :], row_ps[:, f % 2, :, :]).then_inc(copied, 1)


def modulate_stage(k, which, xhat, scale_row, shift_row):
    nc = k.nc
    G = 4
    with ExitStack() as ctx:
        scaled, = sems(nc, ctx, f"mo{which}_scaled")
        block = ctx.enter_context(nc.Block())
        h = xhat[:, :, :].rearrange("p (b t) d -> p b t d", t=TT)
        wide = lambda row, g: row[:, g:g + G, :].unsqueeze(2).to_broadcast([P, G, TT, P])

        @block.vector
        def _(dve):
            for i, g in enumerate(range(0, B, G)):
                nc.vector.tensor_tensor(h[:, g:g + G], h[:, g:g + G], wide(scale_row, g), ALU.mult).then_inc(scaled, 1)
                dve.wait_ge(scaled, i + 1)
                nc.vector.tensor_tensor(h[:, g:g + G], h[:, g:g + G], wide(shift_row, g), ALU.add)


def residual_stage(k, which, y, gate_row):
    nc = k.nc
    G = 4
    with ExitStack() as ctx:
        gated, = sems(nc, ctx, f"re{which}_gated")
        block = ctx.enter_context(nc.Block())
        yb = y[:, :, :].rearrange("p (b t) d -> p b t d", t=TT)
        xb = k.x[:, :, :].rearrange("p (b t) d -> p b t d", t=TT)

        @block.vector
        def _(dve):
            for g in range(0, B, G):
                nc.vector.tensor_tensor(yb[:, g:g + G], yb[:, g:g + G],
                                        gate_row[:, g:g + G, :].unsqueeze(2).to_broadcast([P, G, TT, P]),
                                        ALU.mult).then_inc(gated, 1)

        @block.gpsimd
        def _(pool):
            for i, g in enumerate(range(0, B, G)):
                pool.wait_ge(gated, i + 1)
                nc.gpsimd.tensor_tensor(xb[:, g:g + G], xb[:, g:g + G], yb[:, g:g + G], ALU.add)


def norm_stage(k, which, xhat):
    nc = k.nc
    NG, G = 4, NT // 4
    with ExitStack() as ctx:
        mean = k.sb(ctx, f"ln{which}_mean", [P, NT])
        var = k.sb(ctx, f"ln{which}_var", [P, NT])
        sq = k.sb(ctx, f"ln{which}_sq", [P, 2, G, P])
        centred, squared, summed, meaned, rooted = sems(
            nc, ctx, f"ln{which}_centred ln{which}_squared ln{which}_summed ln{which}_meaned ln{which}_rooted")
        block = ctx.enter_context(nc.Block())

        def scale_group(dve, g):
            s = slice(g * G, (g + 1) * G)
            dve.wait_ge(squared, g + 1)
            nc.vector.tensor_reduce(var[:, s], sq[:, g % 2, :, :], AX.X, ALU.add).then_inc(summed, 1)
            dve.wait_ge(summed, g + 1)
            nc.vector.tensor_scalar(var[:, s], var[:, s], 1.0 / P, LN_EPS, ALU.mult, ALU.add).then_inc(rooted, 1)
            dve.wait_ge(rooted, 3 * g + 2)
            nc.vector.reciprocal(var[:, s], var[:, s]).then_inc(rooted, 1)
            dve.wait_ge(rooted, 3 * g + 3)
            nc.vector.tensor_tensor(xhat[:, s, :], xhat[:, s, :], var[:, s].unsqueeze(2).to_broadcast([P, G, P]),
                                    ALU.mult)

        @block.vector
        def _(dve):
            for g in range(NG):
                s = slice(g * G, (g + 1) * G)
                nc.vector.tensor_reduce(mean[:, s], k.x[:, s, :], AX.X, ALU.add).then_inc(meaned, 1)
                dve.wait_ge(meaned, 2 * g + 1)
                nc.vector.tensor_scalar(mean[:, s], mean[:, s], 1.0 / P, None, ALU.mult).then_inc(meaned, 1)
                dve.wait_ge(meaned, 2 * g + 2)
                nc.vector.tensor_tensor(xhat[:, s, :], k.x[:, s, :], mean[:, s].unsqueeze(2).to_broadcast([P, G, P]),
                                        ALU.subtract).then_inc(centred, 1)
                scale_group(dve, g)

        @block.scalar
        def _(act):
            for g in range(NG):
                act.wait_ge(centred, g + 1)
                if g >= 2:
                    act.wait_ge(summed, g - 1)
                nc.scalar.activation(sq[:, g % 2, :, :], xhat[:, g * G:(g + 1) * G, :], ACT.Square).then_inc(squared, 1)
                act.wait_ge(rooted, 3 * g + 1)
                nc.scalar.activation(var[:, g * G:(g + 1) * G], var[:, g * G:(g + 1) * G], ACT.Sqrt).then_inc(rooted, 1)


def combine_plan():
    sizes = [T + 1]
    while sizes[-1] > 1:
        sizes.append(sizes[-1] // 2)
    up, down = [], []
    for n in range(len(sizes) - 1):
        up.append([(n, 0, 2, n, 1, 2, n + 1, 0, 1, sizes[n + 1])])
    for n in range(len(sizes) - 2, -1, -1):
        evens = (sizes[n] - 1) // 2
        down.append([(n + 1, 0, 1, n, 2, 2, n, 2, 2, evens)] if evens else [])
    return sizes, up, down


def scan_stage(k, xhat, gate_row):
    nc, d = k.nc, k.dram
    sizes, up, down = combine_plan()
    offs = np.concatenate([[0], np.cumsum(sizes)]).astype(int).tolist()
    pieces = []
    for group in up + down:
        for (ln, ls, lstep, rn, rs, rstep, tn, ts, tstep, count) in group:
            for c in range(0, count, 32):
                m = min(32, count - c)
                pieces.append((offs[ln] + ls + c * lstep, lstep, offs[rn] + rs + c * rstep, rstep,
                               offs[tn] + ts + c * tstep, tstep, m))
    nup = sum((c + 31) // 32 for c in sizes[1:])
    odd_copies = {}
    at = nup
    for n in range(len(sizes) - 2, -1, -1):
        odd_copies.setdefault(at, []).append((offs[n + 1], offs[n] + 1, sizes[n + 1]))
        at += ((sizes[n] - 1) // 2 + 31) // 32
    wrote, needs = {}, []
    for i, (l, lst, r, rst, t, tst, m) in enumerate(pieces):
        touched = [l + lst * j for j in range(m)] + [r + rst * j for j in range(m)]
        needs.append(max([wrote.get(e, -1) for e in touched] + [-1]) + 1)
        for j in range(m):
            wrote[t + tst * j] = i
    with ExitStack() as ctx:
        E = k.sb(ctx, "scan_levels", [P, offs[-1], B])
        vT = k.sb(ctx, "scan_vT", [P, B, T])
        Wq = k.sb(ctx, "scan_WqT", [P, P])
        Wv = k.sb(ctx, "scan_WvT", [P, P])
        Wc = k.sb(ctx, "scan_WcT", [P, P])
        idn = k.sb(ctx, "scan_identity", [P, 1])
        hT = k.sb(ctx, "scan_hT", [P, 2, T])
        xs = k.sb(ctx, "scan_xs", [P, 2, TT, P])
        sq = k.sb(ctx, "scan_sq", [P, 2, 512])
        rinv = k.sb(ctx, "scan_rinv", [P, 2, 512])
        log = k.sb(ctx, "scan_log", [P, 2, 512])
        eps = k.sb(ctx, "scan_eps", [P, 1])
        avg = k.sb(ctx, "scan_avg", [P, P])
        qv = k.sb(ctx, "scan_qv", [P, 2, T])
        gy = k.sb(ctx, "scan_gy", [P, 2, TT, P])
        tr_ps = k.ps(ctx, "scan_tr_ps", [P, 2, 512])
        q_ps = k.ps(ctx, "scan_q_ps", [P, 2, 512])
        z_ps = k.ps(ctx, "scan_z_ps", [P, 2, 512])
        m_ps = k.ps(ctx, "scan_m_ps", [P, 2, 512])
        (loaded, staged, turned, hT_ready, proj_ready, q_stored, v_stored, inited, z_ready, sq_ready, mean_ready,
         rinv_ready, combined, qv_ready, y_ready, gated, added, odds_moved, log_ready) = sems(
            nc, ctx, "sc_loaded sc_staged sc_turned sc_hT_ready sc_proj_ready sc_q_stored sc_v_stored sc_inited "
            "sc_z_ready sc_sq_ready sc_mean_ready sc_rinv_ready sc_combined sc_qv_ready sc_y_ready sc_gated sc_added "
            "sc_odds_moved sc_log_ready")
        block = ctx.enter_context(nc.Block())

        @block.sync
        def _(sp):
            sp.dma_start(Wq[:, :], d["WqT"]).then_inc(loaded, 16)
            sp.dma_start(Wv[:, :], d["WvT"]).then_inc(loaded, 16)
            sp.dma_start(Wc[:, :], d["WcT"]).then_inc(loaded, 16)
            sp.dma_start(idn[:, :], d["L0_attn_identity"].rearrange("(p a) -> p a", a=1)).then_inc(loaded, 16)

        @block.gpsimd
        def _(pool):
            for b in range(B):
                if b >= 2:
                    pool.wait_ge(turned, b - 1)
                nc.gpsimd.tensor_copy(xs[:, b % 2, :, :], xhat[:, TT * b:TT * b + TT, :]).then_inc(staged, 1)

        @block.tensor
        def _(pe):
            for b in range(B):
                pe.wait_ge(staged, b + 1)
                if b >= 2:
                    pe.wait_ge(hT_ready, b - 1)
                for t in range(TT):
                    last = nc.tensor.transpose(tr_ps[:, b % 2, t * P:(t + 1) * P], xs[:, b % 2, t, :], k.ident[:, :])
                last.then_inc(turned, 1)
                pe.wait_ge(hT_ready, b + 1)
                pe.wait_ge(loaded, 64)
                if b >= 2:
                    pe.wait_ge(q_stored, b - 1)
                    pe.wait_ge(v_stored, b - 1)
                nc.tensor.matmul(q_ps[:, b % 2, 0:T], Wq[:, :], hT[:, b % 2, :], start=True, stop=True)
                nc.tensor.matmul(z_ps[:, b % 2, 0:T], Wv[:, :], hT[:, b % 2, :], start=True, stop=True)\
                    .then_inc(proj_ready, 1)
            pe.wait_ge(q_stored, B)
            pe.wait_ge(v_stored, B)
            pe.wait_ge(inited, 3)

            def mean_square(i):
                m = pieces[i][6]
                pe.wait_ge(sq_ready, i + 1)
                if i >= 2:
                    pe.wait_ge(rinv_ready, i - 1)
                nc.tensor.matmul(m_ps[:, i % 2, 0:m * B], avg[:, :], sq[:, i % 2, 0:m * B], start=True, stop=True)\
                    .then_inc(mean_ready, 1)

            done = 0
            for i, (l, lst, r, rst, t, tst, m) in enumerate(pieces):
                while needs[i] > done:
                    mean_square(done)
                    done += 1
                if needs[i]:
                    pe.wait_ge(combined, needs[i])
                if i >= 2:
                    pe.wait_ge(combined, i - 1)
                nc.tensor.matmul(z_ps[:, i % 2, 0:m * B], k.PT[:, 0, :], E[:, l:l + lst * (m - 1) + 1:lst, :],
                                 start=True, stop=False)
                nc.tensor.matmul(z_ps[:, i % 2, 0:m * B], k.PT[:, 1, :], E[:, r:r + rst * (m - 1) + 1:rst, :],
                                 start=False, stop=True).then_inc(z_ready, 1)
                while done < i:
                    mean_square(done)
                    done += 1
            mean_square(len(pieces) - 1)
            for b in range(B):
                pe.wait_ge(qv_ready, b + 1)
                if b >= 2:
                    pe.wait_ge(gated, b - 1)
                for t in range(TT):
                    last = nc.tensor.matmul(q_ps[:, b % 2, t * P:(t + 1) * P], qv[:, b % 2, t * P:(t + 1) * P],
                                            Wc[:, :], start=True, stop=True)
                last.then_inc(y_ready, 1)

        @block.scalar
        def _(act):
            for b in range(B):
                act.wait_ge(turned, b + 1)
                if b >= 2:
                    act.wait_ge(proj_ready, b - 1)
                nc.scalar.activation(hT[:, b % 2, :], tr_ps[:, b % 2, 0:T], ACT.Identity,
                                     scale=k.scale1[:, 0, b:b + 1], bias=k.shift[:, 0, b:b + 1]).then_inc(hT_ready, 1)
                act.wait_ge(proj_ready, b + 1)
                nc.scalar.activation(vT[:, b, :], z_ps[:, b % 2, 0:T], ACT.Copy).then_inc(v_stored, 1)

            def inverse_rms(i):
                m = pieces[i][6]
                act.wait_ge(mean_ready, i + 1)
                if i >= 2:
                    act.wait_ge(combined, i - 1)
                nc.scalar.activation(log[:, i % 2, 0:m * B], m_ps[:, i % 2, 0:m * B], ACT.Ln, bias=eps[:, 0:1])\
                    .then_inc(log_ready, 1)
                act.wait_ge(log_ready, i + 1)
                nc.scalar.activation(rinv[:, i % 2, 0:m * B], log[:, i % 2, 0:m * B], ACT.Exp, scale=-0.5)\
                    .then_inc(rinv_ready, 1)

            act.wait_ge(inited, 3)
            finished = 0
            for i, piece in enumerate(pieces):
                m = piece[6]
                act.wait_ge(z_ready, i + 1)
                if i >= 2:
                    act.wait_ge(mean_ready, i - 1)
                nc.scalar.activation(sq[:, i % 2, 0:m * B], z_ps[:, i % 2, 0:m * B], ACT.Square).then_inc(sq_ready, 1)
                if needs[min(i + 1, len(pieces) - 1)] > i or i == len(pieces) - 1:
                    while finished <= i:
                        inverse_rms(finished)
                        finished += 1
                elif finished < i:
                    inverse_rms(finished)
                    finished += 1

        @block.vector
        def _(dve):
            nc.vector.memset(avg[:, :], 1.0 / P).then_inc(inited, 1)
            nc.vector.memset(eps[:, :], 1e-8).then_inc(inited, 1)
            dve.wait_ge(loaded, 64)
            nc.vector.tensor_copy(E[:, 0, :], idn[:, 0:1].to_broadcast([P, B])).then_inc(inited, 1)
            for b in range(B):
                dve.wait_ge(proj_ready, b + 1)
                nc.vector.tensor_copy(E[:, 1:T + 1, b], q_ps[:, b % 2, 0:T]).then_inc(q_stored, 1)
            moved = 0
            for i, (l, lst, r, rst, t, tst, m) in enumerate(pieces):
                dve.wait_ge(rinv_ready, i + 1)
                nc.vector.tensor_tensor(E[:, t:t + tst * (m - 1) + 1:tst, :],
                                        z_ps[:, i % 2, 0:m * B].rearrange("p (n b) -> p n b", b=B),
                                        rinv[:, i % 2, 0:m * B].rearrange("p (n b) -> p n b", b=B),
                                        ALU.mult).then_inc(combined, 1)
                for src, dst, count in odd_copies.get(i + 1, []):
                    dve.wait_ge(combined, i + 1)
                    if moved:
                        dve.wait_ge(odds_moved, moved)
                    nc.vector.tensor_copy(E[:, dst:dst + 2 * count - 1:2, :], E[:, src:src + count, :])\
                        .then_inc(odds_moved, 1)
                    moved += 1
            dve.wait_ge(combined, len(pieces))
            dve.wait_ge(odds_moved, moved)
            dve.wait_ge(v_stored, B)

            def scan_times_v(b):
                if b >= 2:
                    dve.wait_ge(y_ready, b - 1)
                nc.vector.tensor_tensor(qv[:, b % 2, :], E[:, 1:T + 1, b], vT[:, b, :], ALU.mult).then_inc(qv_ready, 1)

            def residual(b):
                dve.wait_ge(y_ready, b + 1)
                nc.vector.tensor_tensor(gy[:, b % 2, :, :], q_ps[:, b % 2, 0:TT * P].rearrange("p (t c) -> p t c", t=TT),
                                        gate_row[:, b:b + 1, :].to_broadcast([P, TT, P]), ALU.mult)\
                    .then_inc(gated, 1)
                dve.wait_ge(gated, b + 1)
                nc.vector.tensor_tensor(k.x[:, TT * b:TT * b + TT, :], k.x[:, TT * b:TT * b + TT, :],
                                        gy[:, b % 2, :, :], ALU.add).then_inc(added, 1)

            scan_times_v(0)
            for b in range(1, B):
                scan_times_v(b)
                residual(b - 1)
            residual(B - 1)


DEPTH, HEADS, HD, WIN = 6, 16, 64, 32
INNER = HEADS * HD
FF = int(P * 4 * 2 / 3)
PAIRS = HEADS // 2
NW = T // WIN
WPT = P // WIN
CHUNKS = 4
MASKED = -1e30
QK_SCALE = 8.0
FILLS = 20
FFILLS = 4
FF_BLOCKS = [(0, P), (P, P), (2 * P, FF - 2 * P)]


class Event:

    def __init__(self, nc, ctx, name, n=1):
        self.sem, self.n = ctx.enter_context(nc.semaphore(name)), n

    def at(self, u, j):
        return (u + 2) * self.n + j

    def start(self, engine):
        engine.sem_inc(self.sem, 2 * self.n)


def transformer_stage(k, z):
    nc, d = k.nc, k.dram
    with ExitStack() as ctx:
        sb = lambda name, shape, dt=F32: k.sb(ctx, "tf_" + name, shape, dt)
        Wqkv = sb("Wqkv", [P, 3 * INNER])
        Wo = sb("Wo", [P, PAIRS, P])
        W1 = sb("W1", [P, 2 * FF])
        W2 = sb("W2", [P, 3, P])
        b1 = sb("b1", [1, 2 * FF])
        b2 = sb("b2", [1, P])
        ln_gb = sb("ln_gb", [P, DEPTH, 2])
        ln_now = sb("ln_now", [P, 2])
        ones = sb("ones", [1, P])
        base = sb("base", [P, 4, TT, HD])
        mult = sb("mult", [P, 4, HD])
        table = sb("table", [P, 4, TT, HD])
        mask32 = sb("mask32", [P, TT, HD])
        mask = sb("mask", [P, TT, HD], BF16)
        identb = sb("identb", [P, P], BF16)
        zu = sb("zu", [P, TT, P])
        xsT = sb("xsT", [P, WIN + T])
        qk = sb("qk", [P, 2, TT, 2 * INNER])
        rot = sb("rot", [P, 2, 512])
        sq = sb("sq", [P, 2, 512])
        ss = sb("ss", [P, 2, TT, 2 * HEADS])
        rn = sb("rn", [P, 2, TT, 2 * HEADS])
        qT = sb("qT", [P, PAIRS, T])
        kT = sb("kT", [P, PAIRS, WIN + T])
        V = sb("V", [P, 2, NW, PAIRS * HD])
        PT = sb("PT", [P, PAIRS, TT, P])
        mx = sb("mx", [P, 2, HEADS])
        den = sb("den", [P, 2, HEADS])
        rden = sb("rden", [P, 2, HEADS])
        ysb = sb("ysb", [P, TT, P])
        flat = qk[:, :, :, :].rearrange("p a t c -> p (a t c)")
        zs = flat[:, 0:NT * P].rearrange("p (n c) -> p n c", c=P)
        o = NT * P
        fsq = flat[:, o:o + 8 * P].rearrange("p (n c) -> p n c", c=P)
        o += 8 * P
        xu = flat[:, o:o + 2 * TT * P].rearrange("p (a t c) -> p a t c", a=2, t=TT)
        o += 2 * TT * P
        mean = flat[:, o:o + NT]
        var = flat[:, o + NT:o + 2 * NT]
        xnT = qT[:, 0, :]
        gel = qT[:, 2:4, :].rearrange("p a c -> p (a c)")
        hm = qT[:, 4:8, :].rearrange("p a c -> p (a c)").rearrange("p (t c) -> p t c", t=TT)
        hT = kT[:, 0:PAIRS, 0:TT * P // 2].rearrange("p a c -> p a c")
        hTs = PT[:, 0:3, :, :]

        psum = k.ps(ctx, "tf_psum", [P, 8, 512])
        proj, trans, score, pv = psum[:, 0:2], psum[:, 2:4], psum[:, 4:6], psum[:, 6:8]
        fa, fg, fy = psum[:, 0:2], psum[:, 4:6], psum[:, 6:8]

        ev = lambda name, n=1: Event(nc, ctx, "tf_" + name, n)
        consts, tables, zeroed, masks_ready, attn_loaded, ff_loaded, ff_small = sems(
            nc, ctx, "tf_consts tf_tables tf_zeroed tf_masks_ready tf_attn_loaded tf_ff_loaded tf_ff_small")
        t_filled, t_copied, f_filled, f_copied = sems(nc, ctx, "tf_t_filled tf_t_copied tf_f_filled tf_f_copied")
        zu_ready, chunk_ready, squared, summed, rotated = ev("zu_ready", 16), ev("chunk", 16), ev("squared", 8), \
            ev("summed", 8), ev("rotated", 8)
        added, v_stored, clamped, rooted, rn_ready, normed = ev("added", 8), ev("v_stored", 8), ev("clamped"), \
            ev("rooted"), ev("rn_ready"), ev("normed", 8)
        scored, maxed, centred, exped, den_sum, den_inv = ev("scored", 2), ev("maxed", 2), ev("centred", 2), \
            ev("exped", 2), ev("den_sum", 2), ev("den_inv", 2)
        pv_done, o_ready, z_added = ev("pv_done", 2), ev("o_ready", 2), ev("z_added")
        shifted, halved, ln_sum, ln_mean, ln_centred, ln_sq, ln_var, ln_root, ln_inv, ln_done = sems(
            nc, ctx, "tf_shifted tf_halved tf_ln_sum tf_ln_mean tf_ln_centred tf_ln_sq tf_ln_var tf_ln_root tf_ln_inv "
            "tf_ln_done")
        xu_ready, hidden, gelued, gated, y_done, y_added = [ev("xu_ready0", 16), ev("xu_ready1", 16)], ev("hidden", 2), ev("gelued", 2), \
            ev("gated", 2), ev("y_done", 2), ev("y_added", 2)
        block = ctx.enter_context(nc.Block())

        @block.sync
        def _(sp):
            sp.dma_start(base[:, :, :, :], d["rope"]).then_inc(consts, 16)
            sp.dma_start(mask32[:, :, :], d["local_mask"]).then_inc(consts, 16)
            sp.dma_start(ln_gb[:, :, :], d["ln_gb"]).then_inc(consts, 16)
            zu_ready.start(sp)
            xu_ready[0].start(sp)
            xu_ready[1].start(sp)

            def load_unit(l, u):
                sp.wait_ge(chunk_ready.sem, chunk_ready.at(l * B + u - 1, 1))
                sp.dma_start(zu[:, :, :], z[:, bass.ds(u * TT, TT), :]).then_inc(zu_ready.sem, 16)

            def load_ff(l, u, p):
                if not isinstance(u, int):
                    sp.wait_ge(f_filled, l * (B * FFILLS) + u * FFILLS - 2 * FFILLS + 4)
                sp.dma_start(xu[:, p, :, :], zs[:, bass.ds(u * TT, TT), :]).then_inc(xu_ready[p].sem, 16)

            with sp.Fori(0, DEPTH) as l:
                sp.wait_ge(z_added.sem, z_added.at(l * B - 1, 1))
                sp.dma_start(Wqkv[:, :], d["L0_ffn_Wqkv"][bass.ds(l, 1), :, :].rearrange("a p n -> p (a n)"))\
                    .then_inc(attn_loaded, 16)
                sp.dma_start(Wo[:, :, :], d["L0_ffn_Wo"][bass.ds(l, 1), :, :].rearrange("a (c p) n -> p (a c) n", p=P))\
                    .then_inc(attn_loaded, 16)
                sp.dma_start(mult[:, :, :], d["rope_scales"][bass.ds(l, 1), :, :].to_broadcast([P, 4, HD]))\
                    .then_inc(attn_loaded, 16)
                sp.wait_ge(y_added.sem, y_added.at(l * B - 1, 2))
                load_unit(l, 0)
                sp.dma_start(W1[:, :], d["L0_ffn_W1"][bass.ds(l, 1), :, :].rearrange("a p n -> p (a n)"))\
                    .then_inc(ff_loaded, 16)
                sp.dma_start(W2[:, :, :], d["W2_padded"][bass.ds(l, 1), :, :].rearrange("a (c p) n -> p (a c) n", p=P))\
                    .then_inc(ff_loaded, 16)
                sp.dma_start(b1[:, :], d["L0_ffn_b1"][bass.ds(l, 1), :]).then_inc(ff_loaded, 16)
                sp.dma_start(b2[:, :], d["L0_ffn_b2"][bass.ds(l, 1), :]).then_inc(ff_loaded, 16)
                with sp.Fori(1, B) as u:
                    load_unit(l, u)
                sp.wait_ge(z_added.sem, z_added.at(l * B + B - 1, 1))
                sp.dma_start(zs[1:P, :, HD:P], z[0:P - 1, :, HD:P]).then_inc(shifted, 16)
                sp.dma_start(zs[0:1, 1:NT:TT, HD:P], z[P - 1:P, 0:NT:TT, HD:P]).then_inc(shifted, 16)
                sp.wait_ge(ln_done, l * 4 + 4)
                load_ff(l, 0, 0)
                load_ff(l, 1, 1)
                with sp.Fori(1, B // 2) as i:
                    load_ff(l, i * 2, 0)
                    load_ff(l, i * 2 + 1, 1)

        @block.gpsimd
        def _(pool):
            for e in (added, normed):
                e.start(pool)
            nc.gpsimd.memset(xsT[:, :], 0.0).then_inc(zeroed, 1)
            nc.gpsimd.memset(kT[:, :, :], 0.0).then_inc(zeroed, 1)
            nc.gpsimd.memset(ones[:, :], 1.0).then_inc(zeroed, 1)

            def rope(l, u, p, g):
                t, c = divmod(g, CHUNKS)
                U = l * B + u
                pool.wait_ge(rotated.sem, rotated.at(U, g + 1))
                x = qk[:, p, t, c * 512:(c + 1) * 512]
                nc.gpsimd.tensor_tensor(x, x, rot[:, g % 2, :], ALU.add).then_inc(added.sem, 1)

            def normalise(l, u, p, g):
                t, c = divmod(g, CHUNKS)
                U = l * B + u
                if g == 0:
                    pool.wait_ge(added.sem, added.at(U, 8))
                    pool.wait_ge(rn_ready.sem, rn_ready.at(U, 1))
                x = qk[:, p, t, c * 512:(c + 1) * 512].rearrange("p (h e) -> p h e", e=HD)
                nc.gpsimd.tensor_tensor(x, x, rn[:, p, t, 8 * c:8 * c + 8].unsqueeze(2).to_broadcast([P, 8, HD]),
                                        ALU.mult).then_inc(normed.sem, 1)

            def prepare(l, u, p):
                for g in range(8):
                    rope(l, u, p, g)
                for g in range(8):
                    normalise(l, u, p, g)

            with pool.Fori(0, DEPTH) as l:
                prepare(l, 0, 0)
                with pool.Fori(0, B // 2 - 1) as i:
                    prepare(l, i * 2 + 1, 1)
                    prepare(l, i * 2 + 2, 0)
                prepare(l, B - 1, 1)

        @block.tensor
        def _(pe):
            for e in (chunk_ready, scored, pv_done, hidden, y_done):
                e.start(pe)

            def bank_free(F):
                pe.wait_ge(t_copied, F + 1)

            def turn_input(l, u, F):
                U = l * B + u
                pe.wait_ge(zu_ready.sem, zu_ready.at(U, 16))
                for t in range(TT):
                    bank_free(F + t)
                    nc.tensor.transpose(trans[:, t, 0:P], zu[:, t, :], k.ident[:, :]).then_inc(t_filled, 1)

            def project(l, u, F, t):
                U = l * B + u
                if t == 0:
                    pe.wait_ge(t_copied, F + 4)
                    pe.wait_ge(attn_loaded, l * 48 + 48)
                for c in range(CHUNKS):
                    g = t * CHUNKS + c
                    if g < 2:
                        pe.wait_ge(v_stored.sem, v_stored.at(U - 1, 7 + g))
                    else:
                        pe.wait_ge(rotated.sem, rotated.at(U, g - 1))
                    nc.tensor.matmul(proj[:, g % 2, :], xsT[:, WIN + t * P:WIN + t * P + P],
                                     Wqkv[:, c * 512:(c + 1) * 512], start=True, stop=True)\
                        .then_inc(chunk_ready.sem, 1)

            def project_v(l, u, w0, w1):
                U = l * B + u
                for w in range(w0, w1):
                    if w < 2:
                        pe.wait_ge(rotated.sem, rotated.at(U, 7 + w))
                    else:
                        pe.wait_ge(v_stored.sem, v_stored.at(U, w - 1))
                    for odd in range(2):
                        rhs = Wqkv[:, 2 * INNER:3 * INNER].rearrange("p (a b e) -> p a b e", b=2, e=HD)[:, :, odd, :]
                        last = nc.tensor.matmul(proj[64 * odd:64 * odd + 64, w % 2, :],
                                                xsT[:, w * WIN:w * WIN + 2 * WIN], rhs, start=True, stop=True)
                    last.then_inc(chunk_ready.sem, 1)

            def turn_qk(l, u, p, F):
                U = l * B + u
                for f in range(8):
                    t, c = divmod(f, CHUNKS)
                    pe.wait_ge(normed.sem, normed.at(U, f + 1))
                    bank_free(F + f)
                    for j in range(4):
                        last = nc.tensor.transpose(trans[:, f % 2, j * P:(j + 1) * P],
                                                   qk[:, p, t, c * 512 + j * P:c * 512 + (j + 1) * P], k.ident[:, :])
                    last.then_inc(t_filled, 1)

            def scores(l, u, p, t, F):
                U = l * B + u
                if t == 0:
                    pe.wait_ge(t_copied, F)
                pe.wait_ge(centred.sem, centred.at(U if t else U - 1, 1 if t else 2))
                for odd in range(2):
                    nc.tensor.matmul(score[:, odd, :], identb[:, :],
                                     mask[:, t:t + 1, :].to_broadcast([P, PAIRS, HD]), start=True, stop=False,
                                     skip_group_check=True)
                for pair in range(PAIRS):
                    for odd in range(2):
                        r = slice(64 * odd, 64 * odd + 64)
                        for w in range(WPT):
                            at = t * P + w * WIN
                            last = nc.tensor.matmul(score[w * WIN:(w + 1) * WIN, odd, pair * HD:(pair + 1) * HD],
                                                    qT[r, pair, at:at + WIN], kT[r, pair, at:at + 2 * WIN],
                                                    start=False, stop=True, skip_group_check=True)
                last.then_inc(scored.sem, 1)

            def turn_probs(l, u, p, t, F):
                U = l * B + u
                pe.wait_ge(exped.sem, exped.at(U, t + 1))
                for f in range(2):
                    bank_free(F + f)
                    for j in range(4):
                        c = (4 * f + j) * P
                        last = nc.tensor.transpose(trans[:, f, j * P:(j + 1) * P], qk[:, p, t, c:c + P], k.ident[:, :])
                    last.then_inc(t_filled, 1)

            def attend(l, u, p, t, F):
                U = l * B + u
                pe.wait_ge(t_copied, F + 4)
                pe.wait_ge(v_stored.sem, v_stored.at(U, 8))
                pe.wait_ge(o_ready.sem, o_ready.at(U if t else U - 1, 1 if t else 2))
                nc.tensor.matmul(pv[:, 0, 0:1], identb[:, :], identb[:, 0:1], start=True, stop=True)
                for pair in range(PAIRS):
                    for odd in range(2):
                        r = slice(64 * odd, 64 * odd + 64)
                        for w in range(WPT):
                            last = nc.tensor.matmul(pv[w * WIN:(w + 1) * WIN, odd, pair * HD:(pair + 1) * HD],
                                                    PT[r, pair, t, w * WIN:(w + 1) * WIN],
                                                    V[r, p, t * WPT + w, pair * HD:(pair + 1) * HD],
                                                    start=True, stop=True)
                last.then_inc(pv_done.sem, 1)

            def turn_out(l, u, p, t, F):
                U = l * B + u
                pe.wait_ge(o_ready.sem, o_ready.at(U, t + 1))
                for f in range(2):
                    bank_free(F + f)
                    for j in range(4):
                        c = INNER + (4 * f + j) * P
                        last = nc.tensor.transpose(trans[:, f, j * P:(j + 1) * P], qk[:, p, t, c:c + P], k.ident[:, :])
                    last.then_inc(t_filled, 1)

            def output(l, u, t, F):
                pe.wait_ge(t_copied, F - t + 2)
                bank_free(F)
                for pair in range(PAIRS):
                    last = nc.tensor.matmul(trans[:, t, 0:P], PT[:, pair, t, :], Wo[:, pair, :],
                                            start=(pair == 0), stop=(pair == PAIRS - 1))
                last.then_inc(t_filled, 1)

            def prologue(l):
                F = l * (B * FILLS)
                turn_input(l, 0, F)
                project(l, 0, F, 0)
                project(l, 0, F, 1)
                project_v(l, 0, 0, NW)
                turn_qk(l, 0, 0, F + 2)

            def body(l, u, p, more):
                F = l * (B * FILLS) + u * FILLS + 10
                scores(l, u, p, 0, F + 0 + 2)
                if more:
                    turn_input(l, u + 1, F)
                    project(l, u + 1, F - 0, 0)
                    F = F + 2
                scores(l, u, p, 1, F)
                if more:
                    project(l, u + 1, F, 1)
                turn_probs(l, u, p, 0, F)
                attend(l, u, p, 0, F)
                if more:
                    project_v(l, u + 1, 0, NW // 2)
                turn_probs(l, u, p, 1, F + 2)
                attend(l, u, p, 1, F + 2)
                if more:
                    project_v(l, u + 1, NW // 2, NW)
                turn_out(l, u, p, 0, F + 4)
                turn_out(l, u, p, 1, F + 6)
                output(l, u, 0, F + 8)
                output(l, u, 1, F + 9)
                if more:
                    turn_qk(l, u + 1, 1 - p, F + 10)

            def turn_ff(l, u, p, F):
                U = l * B + u
                pe.wait_ge(xu_ready[p].sem, xu_ready[p].at(U // 2, 16))
                for t in range(TT):
                    pe.wait_ge(f_copied, F + t + 1)
                    nc.tensor.transpose(trans[:, t, 0:P], xu[:, p, t, :], k.ident[:, :]).then_inc(f_filled, 1)

            def ff_body(l, u, p, more):
                U = l * B + u
                F = l * (B * FFILLS) + u * FFILLS + 2
                for t in range(TT):
                    if t == 0:
                        pe.wait_ge(f_copied, F + 2)
                        pe.wait_ge(ff_loaded, l * 64 + 64)
                    pe.wait_ge(gated.sem, gated.at(U - 1, t + 1))
                    for bank, c in ((fa, 0), (fg, FF)):
                        nc.tensor.matmul(bank[:, t, 0:FF], xnT[:, t * P:(t + 1) * P], W1[:, c:c + FF],
                                         start=True, stop=False)
                        last = nc.tensor.matmul(bank[:, t, 0:FF], ones[:, :], b1[:, c:c + FF], start=False, stop=True)
                    last.then_inc(hidden.sem, 1)
                if more:
                    turn_ff(l, u + 1, 1 - p, F)
                    F = F + 2
                for t in range(TT):
                    pe.wait_ge(gated.sem, gated.at(U, t + 1))
                    pe.wait_ge(f_copied, F + t + 1)
                    for j, (c, m) in enumerate(FF_BLOCKS):
                        last = nc.tensor.transpose(trans[0:m, t, j * P:(j + 1) * P], hm[:, t, c:c + m], k.ident[:, :])
                    last.then_inc(f_filled, 1)
                for t in range(TT):
                    pe.wait_ge(f_copied, F + t + 3)
                    pe.wait_ge(y_added.sem, y_added.at(U - 1, t + 1))
                    for j, (c, m) in enumerate(FF_BLOCKS):
                        nc.tensor.matmul(fy[:, t, 0:P], hTs[0:m, j, t, :], W2[0:m, j, :], start=(j == 0), stop=False)
                    nc.tensor.matmul(fy[:, t, 0:P], ones[:, :], b2[:, :], start=False, stop=True)\
                        .then_inc(y_done.sem, 1)

            pe.wait_ge(zeroed, 3)
            pe.wait_ge(masks_ready, 2)
            with pe.Fori(0, DEPTH) as l:
                prologue(l)
                with pe.Fori(0, B // 2 - 1) as i:
                    body(l, i * 2, 0, True)
                    body(l, i * 2 + 1, 1, True)
                body(l, B - 2, 0, True)
                body(l, B - 1, 1, False)
                turn_ff(l, 0, 0, l * (B * FFILLS))
                with pe.Fori(0, B // 2 - 1) as i:
                    ff_body(l, i * 2, 0, True)
                    ff_body(l, i * 2 + 1, 1, True)
                ff_body(l, B - 2, 0, True)
                ff_body(l, B - 1, 1, False)

        @block.scalar
        def _(act):
            for e in (squared, v_stored, rooted, exped, gelued):
                e.start(act)
            act.sem_inc(t_copied, 2)
            act.sem_inc(f_copied, 2)
            act.wait_ge(zeroed, 3)

            def copy_input(l, u, F):
                for t in range(TT):
                    act.wait_ge(t_filled, F + t + 1)
                    if t == 0:
                        act.wait_ge(chunk_ready.sem, chunk_ready.at(l * B + u - 1, 16))
                    at = WIN + t * P
                    nc.scalar.activation(xsT[0:HD, at:at + P], trans[0:HD, t, 0:P], ACT.Copy)
                    n = P if t == 0 else P - 1
                    nc.scalar.activation(xsT[HD:P, at + 1:at + 1 + n], trans[HD:P, t, 0:n], ACT.Copy)\
                        .then_inc(t_copied, 1)

            def square(l, u, g):
                U = l * B + u
                act.wait_ge(chunk_ready.sem, chunk_ready.at(U, g + 1))
                act.wait_ge(summed.sem, summed.at(U if g >= 2 else U - 1, g - 1 if g >= 2 else 7 + g))
                nc.scalar.activation(sq[:, g % 2, :], proj[:, g % 2, :], ACT.Square).then_inc(squared.sem, 1)

            def store_v(l, u, p, w):
                U = l * B + u
                act.wait_ge(chunk_ready.sem, chunk_ready.at(U, 9 + w))
                nc.scalar.activation(V[:, p, w, :], proj[:, w % 2, :], ACT.Copy).then_inc(v_stored.sem, 1)

            def root(l, u, p):
                U = l * B + u
                act.wait_ge(clamped.sem, clamped.at(U, 1))
                nc.scalar.activation(rn[:, p, :, :], ss[:, p, :, :], ACT.Sqrt).then_inc(rooted.sem, 1)

            def copy_qk(l, u, F):
                for f in range(8):
                    t, c = divmod(f, CHUNKS)
                    act.wait_ge(t_filled, F + f + 1)
                    dst, off = (qT, 0) if c < 2 else (kT, WIN)
                    pair = 4 * (c % 2)
                    nc.scalar.activation(dst[:, pair:pair + 4, off + t * P:off + (t + 1) * P],
                                         trans[:, f % 2, :].rearrange("p (a c) -> p a c", a=4), ACT.Copy)\
                        .then_inc(t_copied, 1)

            def exponential(l, u, p, t):
                U = l * B + u
                act.wait_ge(centred.sem, centred.at(U, t + 1))
                x = qk[:, p, t, 0:INNER]
                nc.scalar.activation(x, x, ACT.Exp, scale=QK_SCALE).then_inc(exped.sem, 1)

            def copy_turned(l, u, t, F):
                for f in range(2):
                    act.wait_ge(t_filled, F + f + 1)
                    nc.scalar.activation(PT[:, 4 * f:4 * f + 4, t, :],
                                         trans[:, f, :].rearrange("p (a c) -> p a c", a=4), ACT.Copy)\
                        .then_inc(t_copied, 1)

            def copy_output(l, u, F):
                for t in range(TT):
                    act.wait_ge(t_filled, F + t + 1)
                    if t == 0:
                        act.wait_ge(z_added.sem, z_added.at(l * B + u - 1, 1))
                    nc.scalar.activation(ysb[:, t, :], trans[:, t, 0:P], ACT.Copy).then_inc(t_copied, 1)

            def prologue(l):
                F = l * (B * FILLS)
                copy_input(l, 0, F)
                for g in range(8):
                    square(l, 0, g)
                for w in range(NW):
                    store_v(l, 0, 0, w)
                root(l, 0, 0)
                copy_qk(l, 0, F + 2)

            def body(l, u, p, more):
                F = l * (B * FILLS) + u * FILLS + 10
                if more:
                    copy_input(l, u + 1, F)
                    F = F + 2
                    for g in range(4):
                        square(l, u + 1, g)
                exponential(l, u, p, 0)
                if more:
                    for g in range(4, 8):
                        square(l, u + 1, g)
                copy_turned(l, u, 0, F)
                exponential(l, u, p, 1)
                if more:
                    for w in range(NW // 2):
                        store_v(l, u + 1, 1 - p, w)
                copy_turned(l, u, 1, F + 2)
                if more:
                    for w in range(NW // 2, NW):
                        store_v(l, u + 1, 1 - p, w)
                    root(l, u + 1, 1 - p)
                copy_turned(l, u, 0, F + 4)
                copy_turned(l, u, 1, F + 6)
                copy_output(l, u, F + 8)
                if more:
                    copy_qk(l, u + 1, F + 10)

            def layer_norm(l):
                act.wait_ge(z_added.sem, z_added.at(l * B + B - 1, 1))
                nc.scalar.activation(zs[:, :, 0:HD], z[:, :, 0:HD], ACT.Copy).then_inc(halved, 1)
                for g in range(4):
                    act.wait_ge(ln_centred, l * 4 + g + 1)
                    if g:
                        act.wait_ge(ln_var, l * 8 + 2 * g - 1)
                    nc.scalar.activation(fsq, zs[:, 8 * g:8 * g + 8, :], ACT.Square).then_inc(ln_sq, 1)
                act.wait_ge(ln_var, l * 8 + 8)
                nc.scalar.activation(var, var, ACT.Sqrt).then_inc(ln_root, 1)

            def copy_ff(l, u, F):
                for t in range(TT):
                    act.wait_ge(f_filled, F + t + 1)
                    if t == 0:
                        act.wait_ge(hidden.sem, hidden.at(l * B + u - 1, 2))
                    nc.scalar.activation(xnT[:, t * P:(t + 1) * P], trans[:, t, 0:P], ACT.Identity,
                                         scale=ln_now[:, 0:1], bias=ln_now[:, 1:2]).then_inc(f_copied, 1)

            def ff_body(l, u, p, more):
                U = l * B + u
                F = l * (B * FFILLS) + u * FFILLS + 2
                for t in range(TT):
                    act.wait_ge(hidden.sem, hidden.at(U, t + 1))
                    act.wait_ge(gated.sem, gated.at(U if t else U - 1, 1 if t else 2))
                    nc.scalar.activation(gel[:, 0:FF], fg[:, t, 0:FF], ACT.Gelu).then_inc(gelued.sem, 1)
                if more:
                    copy_ff(l, u + 1, F)
                    F = F + 2
                for t in range(TT):
                    act.wait_ge(f_filled, F + t + 1)
                    act.wait_ge(y_done.sem, y_done.at(U - 1, t + 1))
                    nc.scalar.activation(hTs[:, 0:2, t, :], trans[:, t, 0:2 * P].rearrange("p (a c) -> p a c", a=2),
                                         ACT.Copy)
                    m = FF_BLOCKS[2][1]
                    nc.scalar.activation(hTs[0:m, 2, t, :], trans[0:m, t, 2 * P:3 * P], ACT.Copy)\
                        .then_inc(f_copied, 1)

            with act.Fori(0, DEPTH) as l:
                prologue(l)
                with act.Fori(0, B // 2 - 1) as i:
                    body(l, i * 2, 0, True)
                    body(l, i * 2 + 1, 1, True)
                body(l, B - 2, 0, True)
                body(l, B - 1, 1, False)
                layer_norm(l)
                act.wait_ge(ff_small, l + 1)
                copy_ff(l, 0, l * (B * FFILLS))
                with act.Fori(0, B // 2 - 1) as i:
                    ff_body(l, i * 2, 0, True)
                    ff_body(l, i * 2 + 1, 1, True)
                ff_body(l, B - 2, 0, True)
                ff_body(l, B - 1, 1, False)

        @block.vector
        def _(dve):
            for e in (summed, rotated, clamped, rn_ready, maxed, centred, den_sum, den_inv, o_ready, gated, y_added,
                      z_added):
                e.start(dve)
            dve.wait_ge(consts, 48)
            nc.vector.tensor_copy(mask[:, :, :], mask32[:, :, :]).then_inc(masks_ready, 1)
            nc.vector.tensor_copy(identb[:, :], k.ident[:, :]).then_inc(masks_ready, 1)

            def rotate(l, u, p, g):
                U = l * B + u
                t, c = divmod(g, CHUNKS)
                kind = 2 * (c // 2)
                dve.wait_ge(squared.sem, squared.at(U, g + 1))
                x = proj[:, g % 2, :].rearrange("p (h e) -> p h e", e=HD)
                cos = table[:, kind, t:t + 1, :].to_broadcast([P, 8, HD])
                sin = table[:, kind + 1, t:t + 1, :].to_broadcast([P, 8, HD])
                nc.vector.tensor_tensor(qk[:, p, t, c * 512:(c + 1) * 512].rearrange("p (h e) -> p h e", e=HD), x, cos,
                                        ALU.mult)
                dve.wait_ge(added.sem, added.at(U if g >= 2 else U - 1, g - 1 if g >= 2 else 7 + g))
                r = rot[:, g % 2, :].rearrange("p (h e) -> p h e", e=HD)
                nc.vector.tensor_tensor(r[:, :, 0:32], x[:, :, 32:64], sin[:, :, 0:32], ALU.mult)
                nc.vector.tensor_tensor(r[:, :, 32:64], x[:, :, 0:32], sin[:, :, 32:64], ALU.mult)\
                    .then_inc(rotated.sem, 1)
                nc.vector.tensor_reduce(ss[:, p, t, 8 * c:8 * c + 8],
                                        sq[:, g % 2, :].rearrange("p (h e) -> p h e", e=HD), AX.X, ALU.add)\
                    .then_inc(summed.sem, 1)

            def inverse_norm(l, u, p):
                U = l * B + u
                dve.wait_ge(summed.sem, summed.at(U, 8))
                nc.vector.tensor_scalar(ss[:, p, :, :], ss[:, p, :, :], 1e-24, None, ALU.max).then_inc(clamped.sem, 1)
                dve.wait_ge(rooted.sem, rooted.at(U, 1))
                nc.vector.reciprocal(rn[:, p, :, :], rn[:, p, :, :]).then_inc(rn_ready.sem, 1)

            def centre(l, u, p, t):
                U = l * B + u
                dve.wait_ge(scored.sem, scored.at(U, t + 1))
                s = score.rearrange("p a (b e) -> p (a b) e", e=HD)
                nc.vector.tensor_reduce(mx[:, t, :], s, AX.X, ALU.max).then_inc(maxed.sem, 1)
                dve.wait_ge(maxed.sem, maxed.at(U, t + 1))
                nc.vector.tensor_tensor(qk[:, p, t, 0:INNER].rearrange("p (b a e) -> p a b e", a=2, e=HD),
                                        score.rearrange("p a (b e) -> p a b e", e=HD),
                                        mx[:, t, :].rearrange("p (a b) -> p a b", a=2).unsqueeze(3)
                                        .to_broadcast([P, 2, PAIRS, HD]), ALU.subtract).then_inc(centred.sem, 1)

            def denominator(l, u, p, t):
                U = l * B + u
                dve.wait_ge(exped.sem, exped.at(U, t + 1))
                nc.vector.tensor_reduce(den[:, t, :], qk[:, p, t, 0:INNER].rearrange("p (h e) -> p h e", e=HD),
                                        AX.X, ALU.add).then_inc(den_sum.sem, 1)
                dve.wait_ge(den_sum.sem, den_sum.at(U, t + 1))
                nc.vector.reciprocal(rden[:, t, :], den[:, t, :]).then_inc(den_inv.sem, 1)

            def normalise_out(l, u, p, t):
                U = l * B + u
                dve.wait_ge(pv_done.sem, pv_done.at(U, t + 1))
                dve.wait_ge(den_inv.sem, den_inv.at(U, t + 1))
                nc.vector.tensor_tensor(qk[:, p, t, INNER:2 * INNER].rearrange("p (b a e) -> p a b e", a=2, e=HD),
                                        pv.rearrange("p a (b e) -> p a b e", e=HD),
                                        rden[:, t, :].rearrange("p (b a) -> p a b", a=2).unsqueeze(3)
                                        .to_broadcast([P, 2, PAIRS, HD]), ALU.mult).then_inc(o_ready.sem, 1)

            def prologue(l):
                dve.wait_ge(attn_loaded, l * 48 + 48)
                nc.vector.tensor_tensor(table[:, :, :, :], base[:, :, :, :],
                                        mult[:, :, :].unsqueeze(2).to_broadcast([P, 4, TT, HD]), ALU.mult)\
                    .then_inc(tables, 1)
                dve.wait_ge(tables, l + 1)
                for g in range(8):
                    rotate(l, 0, 0, g)
                inverse_norm(l, 0, 0)

            def body(l, u, p, more):
                centre(l, u, p, 0)
                if more:
                    for g in range(4):
                        rotate(l, u + 1, 1 - p, g)
                centre(l, u, p, 1)
                denominator(l, u, p, 0)
                if more:
                    for g in range(4, 8):
                        rotate(l, u + 1, 1 - p, g)
                denominator(l, u, p, 1)
                normalise_out(l, u, p, 0)
                if more:
                    inverse_norm(l, u + 1, 1 - p)
                normalise_out(l, u, p, 1)
                add_output(l, u, not more)

            def add_output(l, u, last_unit):
                dve.wait_ge(t_copied, l * (B * FILLS) + u * FILLS + 10 + (10 if last_unit else 12) + 2)
                zt = z[:, bass.ds(u * TT, TT), :] if not isinstance(u, int) else z[:, u * TT:u * TT + TT, :]
                nc.vector.tensor_tensor(zt, zt, ysb[:, :, :], ALU.add).then_inc(z_added.sem, 1)

            def layer_norm(l):
                dve.wait_ge(z_added.sem, z_added.at(l * B + B - 1, 1))
                nc.vector.memset(zs[0:1, 0:NT:TT, HD:P], 0.0).then_inc(ln_sum, 1)
                nc.vector.tensor_copy(ln_now[:, :], ln_gb[:, bass.ds(l, 1), :].rearrange("p a b -> p (a b)"))\
                    .then_inc(ff_small, 1)
                dve.wait_ge(ln_sum, l * 5 + 1)
                dve.wait_ge(halved, l + 1)
                dve.wait_ge(shifted, l * 32 + 32)
                for g in range(4):
                    s = slice(8 * g, 8 * g + 8)
                    nc.vector.tensor_reduce(mean[:, s], zs[:, s, :], AX.X, ALU.add).then_inc(ln_sum, 1)
                    dve.wait_ge(ln_sum, l * 5 + g + 2)
                    nc.vector.tensor_scalar(mean[:, s], mean[:, s], 1.0 / P, None, ALU.mult).then_inc(ln_mean, 1)
                    dve.wait_ge(ln_mean, l * 4 + g + 1)
                    nc.vector.tensor_tensor(zs[:, s, :], zs[:, s, :], mean[:, s].unsqueeze(2).to_broadcast([P, 8, P]),
                                            ALU.subtract).then_inc(ln_centred, 1)
                    dve.wait_ge(ln_sq, l * 4 + g + 1)
                    nc.vector.tensor_reduce(var[:, s], fsq, AX.X, ALU.add).then_inc(ln_var, 1)
                    dve.wait_ge(ln_var, l * 8 + 2 * g + 1)
                    nc.vector.tensor_scalar(var[:, s], var[:, s], 1.0 / P, LN_EPS, ALU.mult, ALU.add)\
                        .then_inc(ln_var, 1)
                dve.wait_ge(ln_root, l + 1)
                nc.vector.reciprocal(var, var).then_inc(ln_inv, 1)
                dve.wait_ge(ln_inv, l + 1)
                for g in range(4):
                    s = slice(8 * g, 8 * g + 8)
                    nc.vector.tensor_tensor(zs[:, s, :], zs[:, s, :], var[:, s].unsqueeze(2).to_broadcast([P, 8, P]),
                                            ALU.mult).then_inc(ln_done, 1)

            def ff_body(l, u, p, more):
                U = l * B + u
                for t in range(TT):
                    dve.wait_ge(gelued.sem, gelued.at(U, t + 1))
                    dve.wait_ge(y_done.sem, y_done.at(U - 1, t + 1))
                    nc.vector.tensor_tensor(hm[:, t, 0:FF], fa[:, t, 0:FF], gel[:, 0:FF], ALU.mult)\
                        .then_inc(gated.sem, 1)
                for t in range(TT):
                    dve.wait_ge(y_done.sem, y_done.at(U, t + 1))
                    zt = z[:, bass.ds(u * TT + t, 1), :].rearrange("p a c -> p (a c)") if not isinstance(u, int) \
                        else z[:, u * TT + t, :]
                    nc.vector.tensor_tensor(zt, zt, fy[:, t, 0:P], ALU.add).then_inc(y_added.sem, 1)

            with dve.Fori(0, DEPTH) as l:
                prologue(l)
                with dve.Fori(0, B // 2 - 1) as i:
                    body(l, i * 2, 0, True)
                    body(l, i * 2 + 1, 1, True)
                body(l, B - 2, 0, True)
                body(l, B - 1, 1, False)
                layer_norm(l)
                with dve.Fori(0, B // 2 - 1) as i:
                    ff_body(l, i * 2, 0, True)
                    ff_body(l, i * 2 + 1, 1, True)
                ff_body(l, B - 2, 0, True)
                ff_body(l, B - 1, 1, False)


QH, QD = 16, 8
S_CHUNKS = 12


def chunk_of(c):
    return (0, 4 * c, 4, P) if c < 4 else (1, 2 * (c - 4), 2, T)


def pairs_of_units(engine, body):
    with engine.Fori(0, B // 2 - 1) as i:
        body(i * 2, 0, True)
        body(i * 2 + 1, 1, True)
    body(B - 2, 0, True)
    body(B - 1, 1, False)


def tile_of(h, u, t):
    if isinstance(u, int):
        return h[:, u * TT + t, :]
    return h[:, bass.ds(u * TT + t, 1), :].rearrange("p a c -> p (a c)")


def mqa_stage(k, h):
    nc, d = k.nc, k.dram
    NC = S_CHUNKS
    with ExitStack() as ctx:
        sb = lambda name, shape, dt=F32: k.sb(ctx, "mq_" + name, shape, dt)
        Wq, Wk, Wv, Wout = sb("Wq", [P, P]), sb("Wk", [P, P]), sb("Wv", [P, QD]), sb("Wout", [P, P])
        bq, bk = sb("bq", [P, 1]), sb("bk", [P, 1])
        bv, bout, ones = sb("bv", [1, QD]), sb("bout", [1, P]), sb("ones", [1, P])
        head_mask = sb("head_mask", [P, QH])
        causal32 = sb("causal32", [P, P])
        mask = sb("mask", [P, 2, 512], BF16)
        identb = sb("identb", [P, P], BF16)
        hu = sb("hu", [P, 2, TT, P])
        hT = sb("hT", [P, T])
        qT = sb("qT", [P, 2, T])
        krep = sb("krep", [P, 2, T])
        kblk = sb("kblk", [P, 2, QH, T])
        V1 = sb("V1", [P, 2, TT, QD + 1])
        prob = sb("prob", [P, 2, 512])
        probT = sb("probT", [P, 2, 4, P])
        mx = sb("mx", [P, 2, 4])
        outT = sb("outT", [QD + 1, TT, QH, P])
        rden = sb("rden", [P, QH])
        o = sb("o", [P, P])
        oT = sb("oT", [P, P])
        psum = k.ps(ctx, "mq_psum", [P, 8, 512])
        score, turned, outp = psum[:, 0:2], psum[:, 2:4], psum[:, 4:6]
        front_ps, back_ps = psum[:, 6], psum[:, 7]
        ev = lambda name, n=1: Event(nc, ctx, "mq_" + name, n)
        loaded, inited, masked = sems(nc, ctx, "mq_loaded mq_inited mq_masked")
        hu_ready = [ev("hu_ready0", 16), ev("hu_ready1", 16)]
        hT_filled, hT_ready, qk_filled, qk_ready, v_filled, v_ready, k_spread = (
            ev(n) for n in "hT_filled hT_ready qk_filled qk_ready v_filled v_ready k_spread".split())
        scored, maxed, centred, exped, t_filled, t_copied, out_done, out_copied = (
            ev(n, NC) for n in "scored maxed centred exped t_filled t_copied out_done out_copied".split())
        back, inverted, o_ready, o_turned, oT_ready, y_done, y_added = (
            ev(n, TT) for n in "back inverted o_ready o_turned oT_ready y_done y_added".split())
        block = ctx.enter_context(nc.Block())

        @block.sync
        def _(sp):
            for e in hu_ready:
                e.start(sp)
            for dst, name in ((Wq, "mqa_Wq"), (Wk, "mqa_Wk_rep"), (Wv, "mqa_Wv"), (Wout, "L1_attn_w_attn_out"),
                              (bq, "mqa_bq"), (bk, "mqa_bk_rep"), (bv, "mqa_bv"), (bout, "mqa_bout"),
                              (head_mask, "head_mask"), (causal32, "causal_mask")):
                sp.dma_start(dst[:, :], d[name]).then_inc(loaded, 16)

            def load(u, p):
                sp.wait_ge(hT_filled.sem, hT_filled.at(u - 2, 1))
                sp.dma_start(hu[:, p, :, :], h[:, bass.ds(u * TT, TT), :]).then_inc(hu_ready[p].sem, 16)

            with sp.Fori(0, B // 2) as i:
                load(i * 2, 0)
                load(i * 2 + 1, 1)

        @block.gpsimd
        def _(pool):
            k_spread.start(pool)
            nc.gpsimd.memset(V1[:, :, :, :], 1.0).then_inc(inited, 1)
            nc.gpsimd.memset(ones[:, :], 1.0).then_inc(inited, 1)
            pool.wait_ge(loaded, 160)

            def spread(u, p):
                pool.wait_ge(qk_ready.sem, qk_ready.at(u, 1))
                nc.gpsimd.tensor_tensor(kblk[:, p, :, :], krep[:, p:p + 1, :].to_broadcast([P, QH, T]),
                                        head_mask[:, :].unsqueeze(2).to_broadcast([P, QH, T]), ALU.mult)\
                    .then_inc(k_spread.sem, 1)

            spread(0, 0)
            pairs_of_units(pool, lambda u, p, more: spread(u + 1, 1 - p) if more else None)

        @block.tensor
        def _(pe):
            for e in (hT_filled, qk_filled, v_filled, scored, t_filled, out_done, back, o_turned, y_done):
                e.start(pe)
            pe.wait_ge(loaded, 160)
            pe.wait_ge(inited, 2)
            pe.wait_ge(masked, 3)

            def front(u, p):
                pe.wait_ge(hu_ready[p].sem, hu_ready[p].at(u // 2, 16))
                pe.wait_ge(v_ready.sem, v_ready.at(u - 1, 1))
                for t in range(TT):
                    last = nc.tensor.transpose(front_ps[:, t * P:(t + 1) * P], hu[:, p, t, :], k.ident[:, :])
                last.then_inc(hT_filled.sem, 1)
                pe.wait_ge(hT_ready.sem, hT_ready.at(u, 1))
                nc.tensor.matmul(front_ps[:, 0:T], Wq[:, :], hT[:, :], start=True, stop=True)
                nc.tensor.matmul(front_ps[:, T:2 * T], Wk[:, :], hT[:, :], start=True, stop=True)\
                    .then_inc(qk_filled.sem, 1)
                pe.wait_ge(qk_ready.sem, qk_ready.at(u, 1))
                for t in range(TT):
                    at = slice(t * QD, (t + 1) * QD)
                    nc.tensor.matmul(front_ps[:, at], hT[:, t * P:(t + 1) * P], Wv[:, :], start=True, stop=False)
                    last = nc.tensor.matmul(front_ps[:, at], ones[:, :], bv[:, :], start=False, stop=True)
                last.then_inc(v_filled.sem, 1)

            def scores(u, p, c):
                t, h0, n, keys = chunk_of(c)
                if c == 0:
                    pe.wait_ge(k_spread.sem, k_spread.at(u, 1))
                pe.wait_ge(centred.sem, centred.at(u, c - 1))
                nc.tensor.matmul(score[:, c % 2, :], identb[:, :], mask[:, t, :], start=True, stop=False,
                                 skip_group_check=True)
                nc.tensor.matmul(score[:, c % 2, :], qT[:, p, t * P:(t + 1) * P], kblk[:, p, h0:h0 + n, 0:keys],
                                 start=False, stop=True, skip_group_check=True).then_inc(scored.sem, 1)

            def turn(u, c):
                pe.wait_ge(exped.sem, exped.at(u, c + 1))
                pe.wait_ge(t_copied.sem, t_copied.at(u, c - 1))
                for j in range(4):
                    last = nc.tensor.transpose(turned[:, c % 2, j * P:(j + 1) * P], prob[:, c % 2, j * P:(j + 1) * P],
                                               k.ident[:, :])
                last.then_inc(t_filled.sem, 1)

            def attend(u, p, c):
                t, h0, n, keys = chunk_of(c)
                pe.wait_ge(t_copied.sem, t_copied.at(u, c + 1))
                pe.wait_ge(out_copied.sem, out_copied.at(u, c - 1))
                blocks = keys // P
                for j in range(blocks):
                    last = nc.tensor.matmul(outp[0:QD + 1, c % 2, 0:n * P], V1[:, p, j, :],
                                            probT[:, c % 2, j:4:blocks, :], start=(j == 0), stop=(j == blocks - 1))
                last.then_inc(out_done.sem, 1)

            def output(u, t):
                pe.wait_ge(out_copied.sem, out_copied.at(u, 4 if t == 0 else NC))
                pe.wait_ge(y_added.sem, y_added.at(u, t))
                for n in range(QH):
                    last = nc.tensor.matmul(back_ps[:, n * (QD + 1):(n + 1) * (QD + 1)], outT[:, t, n, :],
                                            k.ident[0:QD + 1, 0:QD + 1], start=True, stop=True)
                last.then_inc(back.sem, 1)
                pe.wait_ge(o_ready.sem, o_ready.at(u, t + 1))
                nc.tensor.transpose(back_ps[:, 256:256 + P], o[:, :], k.ident[:, :]).then_inc(o_turned.sem, 1)
                pe.wait_ge(oT_ready.sem, oT_ready.at(u, t + 1))
                nc.tensor.matmul(back_ps[:, 0:P], oT[:, :], Wout[:, :], start=True, stop=False)
                nc.tensor.matmul(back_ps[:, 0:P], ones[:, :], bout[:, :], start=False, stop=True)\
                    .then_inc(y_done.sem, 1)

            front(0, 0)

            def body(u, p, more):
                for c in range(NC + 2):
                    if c < NC:
                        scores(u, p, c)
                    if 1 <= c <= NC:
                        turn(u, c - 1)
                    if c >= 2:
                        attend(u, p, c - 2)
                    if c == 8:
                        output(u, 0)
                        if more:
                            front(u + 1, 1 - p)
                output(u, 1)

            pairs_of_units(pe, body)

        @block.scalar
        def _(act):
            for e in (hT_ready, qk_ready, v_ready, exped, t_copied, out_copied, oT_ready):
                e.start(act)
            act.wait_ge(loaded, 160)
            act.wait_ge(inited, 2)

            def front(u, p):
                act.wait_ge(hT_filled.sem, hT_filled.at(u, 1))
                nc.scalar.activation(hT[:, :], front_ps[:, 0:T], ACT.Copy).then_inc(hT_ready.sem, 1)
                act.wait_ge(qk_filled.sem, qk_filled.at(u, 1))
                nc.scalar.activation(qT[:, p, :], front_ps[:, 0:T], ACT.Identity, bias=bq[:, 0:1])
                nc.scalar.activation(krep[:, p, :], front_ps[:, T:2 * T], ACT.Identity, bias=bk[:, 0:1])\
                    .then_inc(qk_ready.sem, 1)
                act.wait_ge(v_filled.sem, v_filled.at(u, 1))
                nc.scalar.activation(V1[:, p, :, 0:QD], front_ps[:, 0:TT * QD].rearrange("p (t e) -> p t e", t=TT),
                                     ACT.Copy).then_inc(v_ready.sem, 1)

            def exponential(u, c):
                act.wait_ge(centred.sem, centred.at(u, c + 1))
                nc.scalar.activation(prob[:, c % 2, :], prob[:, c % 2, :], ACT.Exp, scale=float(QD) ** -0.5)\
                    .then_inc(exped.sem, 1)

            def copy_turned(u, c):
                act.wait_ge(t_filled.sem, t_filled.at(u, c + 1))
                act.wait_ge(out_done.sem, out_done.at(u, c - 1))
                nc.scalar.activation(probT[:, c % 2, :, :], turned[:, c % 2, :].rearrange("p (a c) -> p a c", a=4),
                                     ACT.Copy).then_inc(t_copied.sem, 1)

            def copy_out(u, c):
                t, h0, n, keys = chunk_of(c)
                act.wait_ge(out_done.sem, out_done.at(u, c + 1))
                act.wait_ge(back.sem, back.at(u - 1, t + 1))
                nc.scalar.activation(outT[:, t, h0:h0 + n, :],
                                     outp[0:QD + 1, c % 2, 0:n * P].rearrange("p (a c) -> p a c", a=n), ACT.Copy)\
                    .then_inc(out_copied.sem, 1)

            def output(u, t):
                act.wait_ge(o_turned.sem, o_turned.at(u, t + 1))
                nc.scalar.activation(oT[:, :], back_ps[:, 256:256 + P], ACT.Copy).then_inc(oT_ready.sem, 1)

            front(0, 0)

            def body(u, p, more):
                for c in range(NC + 2):
                    if c < NC:
                        exponential(u, c)
                    if 1 <= c <= NC:
                        copy_turned(u, c - 1)
                    if c >= 2:
                        copy_out(u, c - 2)
                    if c == 8:
                        output(u, 0)
                        if more:
                            front(u + 1, 1 - p)
                output(u, 1)

            pairs_of_units(act, body)

        @block.vector
        def _(dve):
            for e in (maxed, centred, inverted, o_ready, y_added):
                e.start(dve)
            dve.wait_ge(loaded, 160)
            nc.vector.tensor_copy(mask[:, 0, :].rearrange("p (a c) -> p a c", a=4),
                                  causal32[:, :].unsqueeze(1).to_broadcast([P, 4, P])).then_inc(masked, 1)
            wide = mask[:, 1, :].rearrange("p (a b c) -> p a b c", a=2, b=2)
            nc.vector.memset(wide[:, :, 0, :], 0.0)
            nc.vector.tensor_copy(wide[:, :, 1, :], causal32[:, :].unsqueeze(1).to_broadcast([P, 2, P]))\
                .then_inc(masked, 1)
            nc.vector.tensor_copy(identb[:, :], k.ident[:, :]).then_inc(masked, 1)

            def centre(u, c):
                t, h0, n, keys = chunk_of(c)
                dve.wait_ge(scored.sem, scored.at(u, c + 1))
                s = score[:, c % 2, :].rearrange("p (a c) -> p a c", a=n)
                nc.vector.tensor_reduce(mx[:, c % 2, 0:n], s, AX.X, ALU.max).then_inc(maxed.sem, 1)
                dve.wait_ge(t_filled.sem, t_filled.at(u, c - 1))
                dve.wait_ge(maxed.sem, maxed.at(u, c + 1))
                nc.vector.tensor_tensor(prob[:, c % 2, :].rearrange("p (a c) -> p a c", a=n), s,
                                        mx[:, c % 2, 0:n].unsqueeze(2).to_broadcast([P, n, keys]), ALU.subtract)\
                    .then_inc(centred.sem, 1)

            def output(u, t):
                dve.wait_ge(back.sem, back.at(u, t + 1))
                heads = back_ps[:, 0:QH * (QD + 1)].rearrange("p (n e) -> p n e", e=QD + 1)
                nc.vector.reciprocal(rden[:, :].unsqueeze(2), heads[:, :, QD:QD + 1]).then_inc(inverted.sem, 1)
                dve.wait_ge(inverted.sem, inverted.at(u, t + 1))
                nc.vector.tensor_tensor(o[:, :].rearrange("p (n e) -> p n e", e=QD), heads[:, :, 0:QD],
                                        rden[:, :].unsqueeze(2).to_broadcast([P, QH, QD]), ALU.mult)\
                    .then_inc(o_ready.sem, 1)
                dve.wait_ge(y_done.sem, y_done.at(u, t + 1))
                nc.vector.tensor_tensor(tile_of(h, u, t), tile_of(h, u, t), back_ps[:, 0:P], ALU.add)\
                    .then_inc(y_added.sem, 1)

            def body(u, p, more):
                for c in range(NC):
                    centre(u, c)
                    if c == 8:
                        output(u, 0)
                output(u, 1)

            pairs_of_units(dve, body)


DI, DS, DC, DR = 2 * P, 16, 4, P // 16
NB = DI // P
STEPS = DS // 2


def mamba_stage(k, h):
    nc, d = k.nc, k.dram
    with ExitStack() as ctx:
        sb = lambda name, shape, dt=F32: k.sb(ctx, "mb_" + name, shape, dt)
        Win = sb("Win", [P, 2 * DI])
        conv = sb("conv", [P, NB, DC])
        conv_b, b_dt, Dp = sb("conv_b", [P, NB]), sb("b_dt", [P, NB]), sb("Dp", [P, NB])
        A = sb("A", [P, NB, DS])
        Wx = sb("Wx", [P, NB, DR + 2 * DS])
        Wdt = sb("Wdt", [DR, DI])
        Wout = sb("Wout", [P, NB, P])
        sel32, sel = sb("sel32", [3 * 2 * DS, 2 * DS]), sb("sel", [3 * 2 * DS, 2 * DS], BF16)
        hu = sb("hu", [P, 2, TT, P])
        x1T = sb("x1T", [P, T])
        u0 = sb("u0", [P, NB, DC - 1 + T])
        xc = sb("xc", [P, NB, T])
        uu = sb("u", [P, 2, NB, T])
        sres = sb("sres", [P, 2, NB, T])
        dt = sb("dt", [DR, T])
        bc = sb("bc", [2 * DS, T])
        mid = sb("mid", [2 * DS, T], BF16)
        zeros = sb("zeros", [2 * DS, T])
        split = sb("split", [3 * 2 * DS, 2, T], BF16)
        raw = sb("raw", [P, NB, T])
        soft = sb("soft", [P, NB, T])
        delta = sb("delta", [P, 2, NB, T])
        du = sb("du", [P, 2, NB, T])
        decay = sb("decay", [P, 2, 2, NB, T])
        inp = sb("inp", [P, 2, 2, NB, T])
        state = sb("state", [P, 2, 2, NB, T])
        Csb = sb("Csb", [P, 2, 2, T])
        read = sb("read", [P, 2, 2, NB, T])
        yT = sb("yT", [P, NB, T])
        psum = k.ps(ctx, "mb_psum", [P, 8, 512])
        Bps, Cps, y_ps, out_ps = psum[:, 0:2], psum[:, 2:4], psum[:, 4], psum[:, 5]
        fa, fb = psum[:, 6], psum[:, 7]
        ev = lambda name, n=1: Event(nc, ctx, "mb_" + name, n)
        loaded, a_ready, inited, sel_ready = sems(nc, ctx, "mb_loaded mb_a_ready mb_inited mb_sel_ready")
        hu_ready = [ev("hu_ready0", 16), ev("hu_ready1", 16)]
        (turned, x1_ready, xr_done, u0_ready, sres_ready, u_ready, small_done, small_ready, split_ready, dt_done,
         delta_ready, du_ready, out_done, yT_ready) = (ev(n) for n in (
             "turned x1_ready xr_done u0_ready sres_ready u_ready small_done small_ready split_ready dt_done "
             "delta_ready du_ready out_done yT_ready").split())
        conved, splitting, softened = ev("conved", DC), ev("splitting", 4), ev("softened", 4)
        out_added = ev("out_added", TT)
        skipped = ev("skipped")
        B_done, C_done, decay_ready, C_ready, inp_ready, scanned, weighted, summed = (
            ev(n, STEPS) for n in "B_done C_done decay_ready C_ready inp_ready scanned weighted summed".split())
        block = ctx.enter_context(nc.Block())

        @block.sync
        def _(sp):
            for e in hu_ready:
                e.start(sp)
            for dst, name in ((Win[:, :], "L1_attn_w_in"), (conv[:, :, :], "mb_conv"), (conv_b[:, :], "mb_conv_b"),
                              (b_dt[:, :], "mb_b_dt"), (Dp[:, :], "mb_Dp"), (A[:, :, :], "mb_A_log"),
                              (Wx[:, :, :], "mb_Wx"), (Wdt[:, :], "L1_attn_w_dt"), (Wout[:, :, :], "mb_Wout"),
                              (sel32[:, :], "select")):
                sp.dma_start(dst, d[name]).then_inc(loaded, 16)

            def load(u, p):
                sp.wait_ge(turned.sem, turned.at(u - 2, 1))
                sp.dma_start(hu[:, p, :, :], h[:, bass.ds(u * TT, TT), :]).then_inc(hu_ready[p].sem, 16)

            with sp.Fori(0, B // 2) as i:
                load(i * 2, 0)
                load(i * 2 + 1, 1)

        @block.gpsimd
        def _(pool):
            for e in (splitting, split_ready, weighted):
                e.start(pool)
            nc.gpsimd.memset(u0[:, :, 0:DC - 1], 0.0).then_inc(inited, 1)
            nc.gpsimd.memset(decay[:, :, :, :, 0:1], 0.0).then_inc(inited, 1)
            nc.gpsimd.memset(zeros[:, :], 0.0).then_inc(inited, 1)
            pool.wait_ge(inited, 3)

            def split_bc(u, p):
                n = 2 * DS
                pool.wait_ge(small_ready.sem, small_ready.at(u, 1))
                pool.wait_ge(C_done.sem, C_done.at(u - 2, STEPS))
                nc.gpsimd.tensor_tensor(split[0:n, p, :], bc[:, :], zeros[:, :], ALU.add).then_inc(splitting.sem, 1)
                pool.wait_ge(splitting.sem, splitting.at(u, 1))
                nc.gpsimd.tensor_tensor(bc[:, :], bc[:, :], split[0:n, p, :], ALU.subtract)\
                    .then_inc(splitting.sem, 1)
                pool.wait_ge(splitting.sem, splitting.at(u, 2))
                nc.gpsimd.tensor_tensor(mid[:, :], bc[:, :], zeros[:, :], ALU.add).then_inc(splitting.sem, 1)
                pool.wait_ge(splitting.sem, splitting.at(u, 3))
                nc.gpsimd.tensor_tensor(split[n:2 * n, p, :], mid[:, :], zeros[:, :], ALU.add)
                nc.gpsimd.tensor_tensor(bc[:, :], bc[:, :], mid[:, :], ALU.subtract).then_inc(splitting.sem, 1)
                pool.wait_ge(splitting.sem, splitting.at(u, 4))
                nc.gpsimd.tensor_tensor(split[2 * n:3 * n, p, :], bc[:, :], zeros[:, :], ALU.add)\
                    .then_inc(split_ready.sem, 1)
                pool.wait_ge(split_ready.sem, split_ready.at(u, 1))

            def weight(u, m):
                pool.wait_ge(scanned.sem, scanned.at(u, m + 1))
                pool.wait_ge(C_ready.sem, C_ready.at(u, m + 1))
                pool.wait_ge(summed.sem, summed.at(u, m - 1))
                for j in range(2):
                    last = nc.gpsimd.tensor_tensor(read[:, m % 2, j, :, :], state[:, m % 2, j, :, :],
                                                   Csb[:, m % 2, j:j + 1, :].to_broadcast([P, NB, T]), ALU.mult)
                last.then_inc(weighted.sem, 1)

            split_bc(0, 0)

            def body(u, p, more):
                for m in range(STEPS):
                    weight(u, m)
                    if m == 5 and more:
                        split_bc(u + 1, 1 - p)

            pairs_of_units(pool, body)

        @block.tensor
        def _(pe):
            for e in (turned, xr_done, small_done, dt_done, out_done, B_done, C_done, summed):
                e.start(pe)
            pe.wait_ge(loaded, 160)
            pe.wait_ge(sel_ready, 1)

            def front_a(u, p):
                pe.wait_ge(hu_ready[p].sem, hu_ready[p].at(u // 2, 16))
                pe.wait_ge(delta_ready.sem, delta_ready.at(u - 1, 1))
                for t in range(TT):
                    last = nc.tensor.transpose(fa[:, t * P:(t + 1) * P], hu[:, p, t, :], k.ident[:, :])
                last.then_inc(turned.sem, 1)
                pe.wait_ge(x1_ready.sem, x1_ready.at(u, 1))
                for bank, c in ((fa, 0), (fb, DI)):
                    for j in range(NB):
                        last = nc.tensor.matmul(bank[:, j * T:(j + 1) * T], Win[:, c + j * P:c + (j + 1) * P], x1T[:, :],
                                                start=True, stop=True)
                last.then_inc(xr_done.sem, 1)

            def front_b(u, p):
                pe.wait_ge(u_ready.sem, u_ready.at(u, 1))
                pe.wait_ge(sres_ready.sem, sres_ready.at(u, 1))
                for part, lo, n in ((0, DR, 2 * DS), (1, 0, DR)):
                    for j in range(NB):
                        last = nc.tensor.matmul(fa[0:n, part * T:(part + 1) * T], Wx[:, j, lo:lo + n], uu[:, p, j, :],
                                                start=(j == 0), stop=(j == NB - 1))
                last.then_inc(small_done.sem, 1)
                pe.wait_ge(small_ready.sem, small_ready.at(u, 1))
                for j in range(NB):
                    last = nc.tensor.matmul(fb[:, j * T:(j + 1) * T], Wdt[:, j * P:(j + 1) * P], dt[:, :],
                                            start=True, stop=True)
                last.then_inc(dt_done.sem, 1)

            def spread(u, p, m):
                if m == 0:
                    pe.wait_ge(split_ready.sem, split_ready.at(u, 1))
                for bank, first, free, done in ((Bps, 0, inp_ready, B_done), (Cps, DS, C_ready, C_done)):
                    pe.wait_ge(free.sem, free.at(u, m - 1))
                    for j in range(2):
                        n = first + 2 * m + j
                        last = nc.tensor.matmul(bank[:, m % 2, j * T:(j + 1) * T],
                                                sel[:, n:n + 1].to_broadcast([3 * 2 * DS, P]), split[:, p, :],
                                                start=True, stop=True)
                    last.then_inc(done.sem, 1)

            def add_states(u, m):
                pe.wait_ge(weighted.sem, weighted.at(u, m + 1))
                if m == 0:
                    pe.wait_ge(skipped.sem, skipped.at(u - 1, 1))
                for j in range(2):
                    last = nc.tensor.matmul(y_ps[:, :], k.ident[:, :], read[:, m % 2, j, :, :],
                                            start=(m == 0 and j == 0), stop=(m == STEPS - 1 and j == 1),
                                            skip_group_check=True)
                last.then_inc(summed.sem, 1)

            def output(u):
                pe.wait_ge(yT_ready.sem, yT_ready.at(u, 1))
                pe.wait_ge(out_added.sem, out_added.at(u - 1, TT))
                for t in range(TT):
                    for j in range(NB):
                        last = nc.tensor.matmul(out_ps[:, t * P:(t + 1) * P], yT[:, j, t * P:(t + 1) * P],
                                                Wout[:, j, :], start=(j == 0), stop=(j == NB - 1))
                last.then_inc(out_done.sem, 1)

            front_a(0, 0)
            front_b(0, 0)

            def body(u, p, more):
                spread(u, p, 0)
                for m in range(STEPS):
                    if m + 1 < STEPS:
                        spread(u, p, m + 1)
                    if m == 2 and more:
                        front_a(u + 1, 1 - p)
                    if m == 4 and more:
                        front_b(u + 1, 1 - p)
                    add_states(u, m)
                output(u)

            pairs_of_units(pe, body)

        @block.scalar
        def _(act):
            for e in (x1_ready, u0_ready, sres_ready, u_ready, small_ready, softened, decay_ready, C_ready):
                e.start(act)
            act.wait_ge(loaded, 160)
            act.wait_ge(inited, 3)
            nc.scalar.activation(A[:, :, :], A[:, :, :], ACT.Exp).then_inc(a_ready, 1)

            def front_a(u, p):
                act.wait_ge(turned.sem, turned.at(u, 1))
                nc.scalar.activation(x1T[:, :], fa[:, 0:T], ACT.Copy).then_inc(x1_ready.sem, 1)
                act.wait_ge(xr_done.sem, xr_done.at(u, 1))
                act.wait_ge(conved.sem, conved.at(u - 1, DC))
                nc.scalar.activation(u0[:, :, DC - 1:DC - 1 + T], fa.rearrange("p (j t) -> p j t", j=NB), ACT.Copy)\
                    .then_inc(u0_ready.sem, 1)
                act.wait_ge(yT_ready.sem, yT_ready.at(u - 2, 1))
                nc.scalar.activation(sres[:, p, :, :], fb.rearrange("p (j t) -> p j t", j=NB), ACT.Silu)\
                    .then_inc(sres_ready.sem, 1)
                act.wait_ge(conved.sem, conved.at(u, DC))
                for j in range(NB):
                    last = nc.scalar.activation(uu[:, p, j, :], xc[:, j, :], ACT.Silu, bias=conv_b[:, j:j + 1])
                last.then_inc(u_ready.sem, 1)

            def front_b(u, p):
                act.wait_ge(small_done.sem, small_done.at(u, 1))
                act.wait_ge(split_ready.sem, split_ready.at(u - 1, 1))
                nc.scalar.activation(bc[:, :], fa[0:2 * DS, 0:T], ACT.Copy)
                nc.scalar.activation(dt[:, :], fa[0:DR, T:2 * T], ACT.Copy).then_inc(small_ready.sem, 1)
                act.wait_ge(dt_done.sem, dt_done.at(u, 1))
                act.wait_ge(delta_ready.sem, delta_ready.at(u - 1, 1))
                for j in range(NB):
                    last = nc.scalar.activation(raw[:, j, :], fb[:, j * T:(j + 1) * T], ACT.Identity,
                                                bias=b_dt[:, j:j + 1])
                last.then_inc(softened.sem, 1)
                act.wait_ge(softened.sem, softened.at(u, 1))
                nc.scalar.activation(soft[:, :, :], raw[:, :, :], ACT.Abs).then_inc(softened.sem, 1)
                act.wait_ge(softened.sem, softened.at(u, 2))
                nc.scalar.activation(soft[:, :, :], soft[:, :, :], ACT.Exp, scale=-1.0).then_inc(softened.sem, 1)
                act.wait_ge(softened.sem, softened.at(u, 3))
                nc.scalar.activation(soft[:, :, :], soft[:, :, :], ACT.Ln, bias=1.0).then_inc(softened.sem, 1)

            def decays(u, p, m):
                if m == 0:
                    act.wait_ge(delta_ready.sem, delta_ready.at(u, 1))
                act.wait_ge(scanned.sem, scanned.at(u, m - 1))
                for j in range(2):
                    for b in range(NB):
                        last = nc.scalar.activation(decay[:, m % 2, j, b, 1:T], delta[:, p, b, 1:T], ACT.Exp,
                                                    scale=A[:, b, 2 * m + j:2 * m + j + 1])
                last.then_inc(decay_ready.sem, 1)

            def copy_c(u, m):
                act.wait_ge(C_done.sem, C_done.at(u, m + 1))
                act.wait_ge(weighted.sem, weighted.at(u, m - 1))
                nc.scalar.activation(Csb[:, m % 2, :, :], Cps[:, m % 2, :].rearrange("p (j t) -> p j t", j=2),
                                     ACT.Copy).then_inc(C_ready.sem, 1)

            front_a(0, 0)
            front_b(0, 0)
            act.wait_ge(a_ready, 2)

            def body(u, p, more):
                for m in range(STEPS):
                    decays(u, p, m)
                    copy_c(u, m)
                    if m == 2 and more:
                        front_a(u + 1, 1 - p)
                    if m == 4 and more:
                        front_b(u + 1, 1 - p)

            pairs_of_units(act, body)

        @block.vector
        def _(dve):
            for e in (conved, delta_ready, du_ready, inp_ready, scanned, yT_ready, skipped, out_added):
                e.start(dve)
            dve.wait_ge(loaded, 160)
            nc.vector.tensor_copy(sel[:, :], sel32[:, :]).then_inc(sel_ready, 1)
            dve.wait_ge(a_ready, 1)
            nc.vector.tensor_scalar(A[:, :, :], A[:, :, :], -1.0, None, ALU.mult).then_inc(a_ready, 1)

            def front_a(u, p):
                dve.wait_ge(u0_ready.sem, u0_ready.at(u, 1))
                dve.wait_ge(u_ready.sem, u_ready.at(u - 1, 1))
                for tap in range(DC):
                    if tap:
                        dve.wait_ge(conved.sem, conved.at(u, tap))
                    for j in range(NB):
                        src, w = u0[:, j, tap:tap + T], conv[:, j, tap:tap + 1]
                        if tap == 0:
                            last = nc.vector.tensor_scalar(xc[:, j, :], src, w, None, ALU.mult)
                        else:
                            last = nc.vector.scalar_tensor_tensor(out=xc[:, j, :], in0=src, scalar=w, in1=xc[:, j, :],
                                                                  op0=ALU.mult, op1=ALU.add)
                    last.then_inc(conved.sem, 1)

            def front_b(u, p):
                dve.wait_ge(softened.sem, softened.at(u, 4))
                nc.vector.scalar_tensor_tensor(out=delta[:, p, :, :], in0=raw[:, :, :], scalar=0.0, in1=soft[:, :, :],
                                               op0=ALU.max, op1=ALU.add).then_inc(delta_ready.sem, 1)
                dve.wait_ge(delta_ready.sem, delta_ready.at(u, 1))
                nc.vector.tensor_tensor(du[:, p, :, :], delta[:, p, :, :], uu[:, p, :, :], ALU.mult)\
                    .then_inc(du_ready.sem, 1)

            def step(u, p, m):
                if m == 0:
                    dve.wait_ge(du_ready.sem, du_ready.at(u, 1))
                dve.wait_ge(B_done.sem, B_done.at(u, m + 1))
                for j in range(2):
                    last = nc.vector.tensor_tensor(inp[:, m % 2, j, :, :], du[:, p, :, :],
                                                   Bps[:, m % 2, j * T:(j + 1) * T].unsqueeze(1)
                                                   .to_broadcast([P, NB, T]), ALU.mult)
                last.then_inc(inp_ready.sem, 1)
                dve.wait_ge(inp_ready.sem, inp_ready.at(u, m + 1))
                dve.wait_ge(decay_ready.sem, decay_ready.at(u, m + 1))
                dve.wait_ge(weighted.sem, weighted.at(u, m - 1))
                flat = lambda x: x[:, m % 2].rearrange("p j b t -> p (j b t)")
                nc.vector.tensor_tensor_scan(flat(state), flat(decay), flat(inp), 0.0, ALU.mult, ALU.add)\
                    .then_inc(scanned.sem, 1)

            def finish(u, p):
                dve.wait_ge(summed.sem, summed.at(u, STEPS))
                dve.wait_ge(out_done.sem, out_done.at(u - 1, 1))
                for j in range(NB):
                    last = nc.vector.scalar_tensor_tensor(out=yT[:, j, :], in0=uu[:, p, j, :], scalar=Dp[:, j:j + 1],
                                                          in1=y_ps[:, j * T:(j + 1) * T], op0=ALU.mult, op1=ALU.add)
                last.then_inc(skipped.sem, 1)
                dve.wait_ge(skipped.sem, skipped.at(u, 1))
                nc.vector.tensor_tensor(yT[:, :, :], yT[:, :, :], sres[:, p, :, :], ALU.mult)\
                    .then_inc(yT_ready.sem, 1)

            def add_output(u):
                for t in range(TT):
                    dve.wait_ge(out_done.sem, out_done.at(u, 1))
                    nc.vector.tensor_tensor(tile_of(h, u, t), tile_of(h, u, t), out_ps[:, t * P:(t + 1) * P], ALU.add)\
                        .then_inc(out_added.sem, 1)

            front_a(0, 0)
            front_b(0, 0)

            def body(u, p, more):
                for m in range(STEPS):
                    step(u, p, m)
                    if m == 2 and more:
                        front_a(u + 1, 1 - p)
                    if m == 5 and more:
                        front_b(u + 1, 1 - p)
                finish(u, p)
                add_output(u)

            pairs_of_units(dve, body)


NE, MR, NS, MS = 16, P // 4, 2, P // 2
HID = NE * MR + NS * MS
HB = HID // P


def moe_stage(k, h, gate_row):
    nc, d = k.nc, k.dram
    NR = NE * MR
    with ExitStack() as ctx:
        sb = lambda name, shape, dt=F32: k.sb(ctx, "me_" + name, shape, dt)
        Wg, Wu = sb("Wg", [P, NR]), sb("Wu", [P, NR])
        Wsh = sb("Wsh", [P, 2 * NS * MS + NE])
        Wd = sb("Wd", [P, HB, P])
        iota = sb("iota", [P, NE])
        hu = sb("hu", [P, 2, TT, P])
        hT = sb("hT", [P, 2, T])
        prob = sb("prob", [P, 2, NE])
        nmax, tot = sb("nmax", [P, 2]), sb("tot", [P, 2])
        top = sb("top", [P, 2, 8])
        idx = sb("idx", [P, 2, 8], mybir.dt.uint32)
        idxf = sb("idxf", [P, 2, 2])
        wsum = sb("wsum", [P, 2])
        weight = sb("weight", [P, 2, 2])
        comb = sb("comb", [P, 2, NE])
        turnstile = sb("turnstile", [P, 1])
        one = sb("one", [P, 2, NE])
        sg = sb("sg", [P, 2, HID])
        hid = sb("hid", [P, 2, HID])
        hidT = sb("hidT", [P, 2, HB, P])
        gy = sb("gy", [P, 2, P])
        psum = k.ps(ctx, "me_psum", [P, 8, 512])
        g_ps, u_ps, s_ps, r_ps, t_ps, t2_ps, tr_ps, y_ps = (psum[:, i] for i in range(8))
        ev = lambda name, n=TT: Event(nc, ctx, "me_" + name, n)
        loaded, = sems(nc, ctx, "me_loaded")
        hu_ready = [ev("hu_ready0", 16), ev("hu_ready1", 16)]
        (turned, hT_ready) = ev("turned", 1), ev("hT_ready", 1)
        (routed, up_done, nmax_ready, exped, inverted, probs_ready, topped, indexed, indexf, wsummed, winv, weighted,
         combed, silued, multiplied, scaled, hid_turned, hid_copied, y_done, gated, added) = (ev(n) for n in (
             "routed up_done nmax_ready exped inverted probs_ready topped indexed indexf wsummed winv weighted "
             "combed silued multiplied scaled hid_turned hid_copied y_done gated added").split())
        chain = ev("chain", 2 * TT)
        block = ctx.enter_context(nc.Block())

        @block.sync
        def _(sp):
            for e in hu_ready:
                e.start(sp)
            for dst, name in ((Wg[:, :], "moe_Wg"), (Wu[:, :], "moe_Wu"), (Wsh[:, :], "moe_Wsh"),
                              (Wd[:, :, :], "moe_Wd"), (iota[:, :], "expert_numbers")):
                sp.dma_start(dst, d[name]).then_inc(loaded, 16)

            def load(u, p):
                sp.wait_ge(turned.sem, turned.at(u - 2, 1))
                sp.dma_start(hu[:, p, :, :], h[:, bass.ds(u * TT, TT), :]).then_inc(hu_ready[p].sem, 16)

            with sp.Fori(0, B // 2) as i:
                load(i * 2, 0)
                load(i * 2 + 1, 1)

        @block.tensor
        def _(pe):
            for e in (turned, routed, up_done, hid_turned, y_done):
                e.start(pe)
            pe.wait_ge(loaded, 80)

            def turn(u, p):
                pe.wait_ge(hu_ready[p].sem, hu_ready[p].at(u // 2, 16))
                pe.wait_ge(hT_ready.sem, hT_ready.at(u - 1, 1))
                for t in range(TT):
                    last = nc.tensor.transpose(tr_ps[:, t * P:(t + 1) * P], hu[:, p, t, :], k.ident[:, :])
                last.then_inc(turned.sem, 1)

            def experts(u, p, t):
                pe.wait_ge(hT_ready.sem, hT_ready.at(u, 1))
                x = hT[:, p, t * P:(t + 1) * P]
                pe.wait_ge(probs_ready.sem, probs_ready.at(u, t))
                nc.tensor.matmul(r_ps[:, 0:NE], x, Wsh[:, 2 * P:2 * P + NE], start=True, stop=True)\
                    .then_inc(routed.sem, 1)
                pe.wait_ge(multiplied.sem, multiplied.at(u, t))
                nc.tensor.matmul(g_ps[:, 0:NR], x, Wg[:, :], start=True, stop=True)
                nc.tensor.matmul(s_ps[:, 0:P], x, Wsh[:, 0:P], start=True, stop=True)
                nc.tensor.matmul(u_ps[:, 0:NR], x, Wu[:, :], start=True, stop=True)
                nc.tensor.matmul(t2_ps[:, P:2 * P], x, Wsh[:, P:2 * P], start=True, stop=True)\
                    .then_inc(up_done.sem, 1)

            def down(u, t):
                pe.wait_ge(scaled.sem, scaled.at(u, t + 1))
                pe.wait_ge(hid_copied.sem, hid_copied.at(u, t))
                for j in range(4):
                    nc.tensor.transpose(t_ps[:, j * P:(j + 1) * P], hid[:, t, j * P:(j + 1) * P], k.ident[:, :])
                nc.tensor.transpose(y_ps[:, P:2 * P], hid[:, t, 4 * P:5 * P], k.ident[:, :]).then_inc(hid_turned.sem, 1)
                pe.wait_ge(hid_copied.sem, hid_copied.at(u, t + 1))
                for j in range(HB):
                    last = nc.tensor.matmul(y_ps[:, 0:P], hidT[:, t, j, :], Wd[:, j, :], start=(j == 0),
                                            stop=(j == HB - 1))
                last.then_inc(y_done.sem, 1)

            turn(0, 0)

            def body(u, p, more):
                experts(u, p, 0)
                if more:
                    turn(u + 1, 1 - p)
                experts(u, p, 1)
                for t in range(TT):
                    pe.wait_ge(gated.sem, gated.at(u, t))
                    down(u, t)

            pairs_of_units(pe, body)

        @block.scalar
        def _(act):
            for e in (hT_ready, exped, silued, hid_copied):
                e.start(act)

            def copy_turned(u, p):
                act.wait_ge(turned.sem, turned.at(u, 1))
                act.wait_ge(up_done.sem, up_done.at(u - 2, TT))
                nc.scalar.activation(hT[:, p, :], tr_ps[:, 0:T], ACT.Copy).then_inc(hT_ready.sem, 1)

            def route(u, t):
                act.wait_ge(nmax_ready.sem, nmax_ready.at(u, t + 1))
                nc.scalar.activation(prob[:, t, :], r_ps[:, 0:NE], ACT.Exp, bias=nmax[:, t:t + 1],
                                     accum_out=tot[:, t:t + 1]).then_inc(exped.sem, 1)

            def silu(u, t):
                act.wait_ge(up_done.sem, up_done.at(u, t + 1))
                nc.scalar.activation(sg[:, t, 0:NR], g_ps[:, 0:NR], ACT.Silu)
                nc.scalar.activation(sg[:, t, NR:HID], s_ps[:, 0:P], ACT.Silu).then_inc(silued.sem, 1)

            def copy_hidden(u, t):
                act.wait_ge(hid_turned.sem, hid_turned.at(u, t + 1))
                nc.scalar.activation(hidT[:, t, 0:4, :], t_ps.rearrange("p (a c) -> p a c", a=4), ACT.Copy)
                nc.scalar.activation(hidT[:, t, 4, :], y_ps[:, P:2 * P], ACT.Copy).then_inc(hid_copied.sem, 1)

            copy_turned(0, 0)

            def body(u, p, more):
                route(u, 0)
                if more:
                    copy_turned(u + 1, 1 - p)
                silu(u, 0)
                route(u, 1)
                silu(u, 1)
                copy_hidden(u, 0)
                copy_hidden(u, 1)

            pairs_of_units(act, body)

        @block.vector
        def _(dve):
            for e in (nmax_ready, inverted, probs_ready, topped, indexed, indexf, wsummed, winv, weighted, combed,
                      multiplied, scaled, gated, added, chain):
                e.start(dve)
            dve.wait_ge(loaded, 80)

            def route(u, t):
                dve.wait_ge(routed.sem, routed.at(u, t + 1))
                nc.vector.tensor_reduce(nmax[:, t:t + 1], r_ps[:, 0:NE], AX.X, ALU.max, negate=True)\
                    .then_inc(nmax_ready.sem, 1)
                dve.wait_ge(exped.sem, exped.at(u, t + 1))
                nc.vector.reciprocal(tot[:, t:t + 1], tot[:, t:t + 1]).then_inc(inverted.sem, 1)
                dve.wait_ge(inverted.sem, inverted.at(u, t + 1))
                nc.vector.tensor_scalar(prob[:, t, :], prob[:, t, :], tot[:, t:t + 1], None, ALU.mult)\
                    .then_inc(probs_ready.sem, 1)
                dve.wait_ge(probs_ready.sem, probs_ready.at(u, t + 1))
                nc.vector.tensor_scalar(turnstile[:, 0:1], prob[:, t, 0:1], 1.0, None, ALU.mult)
                nc.vector.max(top[:, t, :], prob[:, t, :]).then_inc(topped.sem, 1)
                dve.wait_ge(topped.sem, topped.at(u, t + 1))
                nc.vector.tensor_scalar(wsum[:, t:t + 1], top[:, t, 0:1], top[:, t, 1:2], 1e-9, ALU.add, ALU.add)\
                    .then_inc(wsummed.sem, 1)
                dve.wait_ge(wsummed.sem, wsummed.at(u, t + 1))
                nc.vector.reciprocal(wsum[:, t:t + 1], wsum[:, t:t + 1]).then_inc(winv.sem, 1)
                nc.vector.max_index(idx[:, t, :], top[:, t, :], prob[:, t, :]).then_inc(indexed.sem, 1)
                dve.wait_ge(indexed.sem, indexed.at(u, t + 1))
                nc.vector.tensor_copy(idxf[:, t, :], idx[:, t, 0:2]).then_inc(indexf.sem, 1)
                dve.wait_ge(winv.sem, winv.at(u, t + 1))
                nc.vector.tensor_scalar(weight[:, t, :], top[:, t, 0:2], wsum[:, t:t + 1], None, ALU.mult)\
                    .then_inc(weighted.sem, 1)
                dve.wait_ge(weighted.sem, weighted.at(u, t + 1))
                dve.wait_ge(indexf.sem, indexf.at(u, t + 1))
                nc.vector.tensor_scalar(comb[:, t, :], iota[:, :], idxf[:, t, 0:1], weight[:, t, 0:1],
                                        ALU.is_equal, ALU.mult).then_inc(chain.sem, 1)
                nc.vector.tensor_scalar(one[:, t, :], iota[:, :], idxf[:, t, 1:2], weight[:, t, 1:2],
                                        ALU.is_equal, ALU.mult).then_inc(chain.sem, 1)
                dve.wait_ge(chain.sem, chain.at(u, 2 * t + 2))
                nc.vector.tensor_tensor(comb[:, t, :], comb[:, t, :], one[:, t, :], ALU.add).then_inc(combed.sem, 1)

            def gate_hidden(u, t):
                dve.wait_ge(silued.sem, silued.at(u, t + 1))
                dve.wait_ge(hid_turned.sem, hid_turned.at(u - 1, t + 1))
                nc.vector.tensor_tensor(hid[:, t, 0:NR], u_ps[:, 0:NR], sg[:, t, 0:NR], ALU.mult)
                nc.vector.tensor_tensor(hid[:, t, NR:HID], t2_ps[:, P:2 * P], sg[:, t, NR:HID], ALU.mult)\
                    .then_inc(multiplied.sem, 1)
                dve.wait_ge(multiplied.sem, multiplied.at(u, t + 1))
                dve.wait_ge(combed.sem, combed.at(u, t + 1))
                x = hid[:, t, 0:NR].rearrange("p (e m) -> p e m", e=NE)
                nc.vector.tensor_tensor(x, x, comb[:, t, :].unsqueeze(2).to_broadcast([P, NE, MR]), ALU.mult)\
                    .then_inc(scaled.sem, 1)

            def residual(u, t):
                dve.wait_ge(y_done.sem, y_done.at(u, t + 1))
                row = gate_row[:, u, :] if isinstance(u, int) else \
                    gate_row[:, bass.ds(u, 1), :].rearrange("p a c -> p (a c)")
                nc.vector.tensor_tensor(gy[:, t, :], y_ps[:, 0:P], row, ALU.mult).then_inc(gated.sem, 1)
                dve.wait_ge(gated.sem, gated.at(u, t + 1))
                nc.vector.tensor_tensor(tile_of(k.x, u, t), tile_of(k.x, u, t), gy[:, t, :], ALU.add)\
                    .then_inc(added.sem, 1)

            def body(u, p, more):
                for t in range(TT):
                    route(u, t)
                    gate_hidden(u, t)
                for t in range(TT):
                    residual(u, t)

            pairs_of_units(dve, body)


def store_stage(k):
    nc = k.nc
    with ExitStack() as ctx:
        stored, = sems(nc, ctx, "st_stored")
        block = ctx.enter_context(nc.Block())

        @block.sync
        def _(sp):
            sp.dma_start(k.out.rearrange("b (t p) d -> p (b t) d", p=P), k.x[:, :, :]).then_inc(stored, 16)
            sp.wait_ge(stored, 16)


def build(nc, dram, out):
    with ExitStack() as ctx:
        k = Kernel(nc, dram, out, ctx)
        k.x = k.sb(ctx, "x", [P, NT, P])
        k.ident = k.sb(ctx, "ident", [P, P])
        k.scale1 = k.sb(ctx, "mod_scale", [P, 4, B])
        k.shift = k.sb(ctx, "mod_shift", [P, 4, B])
        k.gate = k.sb(ctx, "mod_gate", [P, 4, B])
        setup_stage(k)
        with ExitStack() as first:
            k.PT = k.sb(first, "polar_PT", [P, 2, P])
            xhat = k.sb(first, "xhat0", [P, NT, P])
            polar_stage(k)
            gate_row = k.sb(first, "gate_row0", [P, B, P])
            rows_stage(k, 0, [(k.gate[:, 0, :], gate_row)])
            norm_stage(k, 0, xhat)
            scan_stage(k, xhat, gate_row)
        with ExitStack() as second:
            z = k.sb(second, "z", [P, NT, P])
            with ExitStack() as rows:
                scale_row = k.sb(rows, "scale_row1", [P, B, P])
                shift_row = k.sb(rows, "shift_row1", [P, B, P])
                rows_stage(k, 1, [(k.scale1[:, 1, :], scale_row), (k.shift[:, 1, :], shift_row)])
                norm_stage(k, 1, z)
                modulate_stage(k, 1, z, scale_row, shift_row)
            transformer_stage(k, z)
            with ExitStack() as rows:
                gate_row = k.sb(rows, "gate_row1", [P, B, P])
                rows_stage(k, 11, [(k.gate[:, 1, :], gate_row)])
                residual_stage(k, 1, z, gate_row)
        clear_released_semaphores(nc)
        with ExitStack() as third:
            y = k.sb(third, "y", [P, NT, P])
            with ExitStack() as rows:
                scale_row = k.sb(rows, "scale_row2", [P, B, P])
                shift_row = k.sb(rows, "shift_row2", [P, B, P])
                rows_stage(k, 2, [(k.scale1[:, 2, :], scale_row), (k.shift[:, 2, :], shift_row)])
                norm_stage(k, 2, y)
                modulate_stage(k, 2, y, scale_row, shift_row)
            mqa_stage(k, y)
            clear_released_semaphores(nc)
            mamba_stage(k, y)
            with ExitStack() as rows:
                gate_row = k.sb(rows, "gate_row2", [P, B, P])
                rows_stage(k, 12, [(k.gate[:, 2, :], gate_row)])
                residual_stage(k, 2, y, gate_row)
        clear_released_semaphores(nc)
        with ExitStack() as fourth:
            y = k.sb(fourth, "y3", [P, NT, P])
            gate_row = k.sb(fourth, "gate_row3", [P, B, P])
            with ExitStack() as rows:
                scale_row = k.sb(rows, "scale_row3", [P, B, P])
                shift_row = k.sb(rows, "shift_row3", [P, B, P])
                rows_stage(k, 3, [(k.scale1[:, 3, :], scale_row), (k.shift[:, 3, :], shift_row),
                                  (k.gate[:, 3, :], gate_row)])
                norm_stage(k, 3, y)
                modulate_stage(k, 3, y, scale_row, shift_row)
            moe_stage(k, y, gate_row)
        store_stage(k)


def shape_constants():
    f = np.float32
    half = np.arange(0, HD, 2, dtype=f)
    inv_freq = f(1.0) / np.power(f(10000.0), half / f(HD))
    tok = np.arange(T, dtype=f)
    freqs = tok[:, None] * inv_freq[None, :]
    base_scale = (half + f(0.4 * HD)) / f(1.4 * HD)
    scale = np.power(base_scale[None, :], ((tok - f(T // 2)) / f(WIN // 2))[:, None])
    cos, sin = np.cos(freqs), np.sin(freqs)
    both = lambda x, y: np.concatenate([x, y], axis=1)
    inv = f(1.0) / scale
    rope = np.stack([both(cos * scale, cos * scale), both(-sin * scale, sin * scale),
                     both(cos * inv, cos * inv), both(-sin * inv, sin * inv)])
    rope = rope.reshape(4, TT, P, HD).transpose(2, 0, 1, 3).astype(f)
    i = np.arange(P)[:, None] % WIN
    j = np.arange(2 * WIN)[None, :]
    open_ = (j - WIN <= i) & (i <= j)
    first = open_ & ((np.arange(P)[:, None] >= WIN) | (j >= WIN))
    local = np.stack([np.where(first, 0, MASKED), np.where(open_, 0, MASKED)], axis=1).astype(f)
    causal = np.where(np.arange(P)[None, :] <= np.arange(P)[:, None], 0, MASKED).astype(f)
    heads = (np.arange(P)[:, None] // QD == np.arange(QH)[None, :]).astype(f)
    select = np.tile(np.eye(2 * DS, dtype=f), (3, 1))
    numbers = np.tile(np.arange(NE, dtype=f), (P, 1))
    return {"ident": np.eye(P, dtype=f), "rope": rope, "local_mask": local, "causal_mask": causal,
            "head_mask": heads, "select": select, "expert_numbers": numbers}


def kernel(**inputs):
    import concourse.bacc as _bacc
    from concourse.bass_utils import run_bass_kernel_spmd as _run

    nc = _bacc.Bacc("TRN2", target_bir_lowering=False, num_devices=1)
    a = {name: np.asarray(value) for name, value in inputs.items()}
    arrays = {}
    arrays["L0_attn_x"] = a["L0_attn_x"]
    arrays["cT"] = np.stack([a["L0_c"].T, a["L1_c"].T], axis=1)
    for name in ("L0_wmod", "L1_wmod", "L0_attn_Wp1", "L0_attn_Wp2", "L0_attn_identity"):
        arrays[name] = a[name]
    for name, source in (("Wp1T", "L0_attn_Wp1"), ("Wp2T", "L0_attn_Wp2"), ("WqT", "L0_attn_Wq"),
                         ("WvT", "L0_attn_Wv"), ("WcT", "L0_attn_Wc")):
        arrays[name] = a[source].T
    for name in ("L0_ffn_Wqkv", "L0_ffn_Wo", "L0_ffn_W1", "L0_ffn_b1", "L0_ffn_b2"):
        arrays[name] = a[name]
    arrays["W2_padded"] = np.pad(a["L0_ffn_W2"], ((0, 0), (0, 3 * P - FF), (0, 0)))
    arrays["ln_gb"] = np.stack([a["L0_ffn_ln_g"].T, a["L0_ffn_ln_b"].T], axis=2)
    qs, ks = a["L0_ffn_q_scale"], a["L0_ffn_k_scale"]
    arrays["rope_scales"] = np.stack([qs, np.roll(qs, HD // 2, axis=1), ks, np.roll(ks, HD // 2, axis=1)], axis=1)
    w, bias = a["L1_attn_wqkv"], a["L1_attn_bqkv"]
    arrays.update(mqa_Wq=w[:, :P], mqa_Wk_rep=np.tile(w[:, P:P + QD], (1, QH)), mqa_Wv=w[:, P + QD:],
                  mqa_bq=bias[:P, None], mqa_bk_rep=np.tile(bias[P:P + QD], QH)[:, None], mqa_bv=bias[None, P + QD:],
                  mqa_bout=a["L1_attn_b_attn_out"][None, :], L1_attn_w_attn_out=a["L1_attn_w_attn_out"])
    blocks = lambda v: v.reshape(NB, P, -1).transpose(1, 0, 2)
    arrays.update(L1_attn_w_in=a["L1_attn_w_in"], mb_conv=blocks(a["L1_attn_conv_w"]),
                  mb_conv_b=blocks(a["L1_attn_conv_b"])[:, :, 0], mb_b_dt=blocks(a["L1_attn_b_dt"])[:, :, 0],
                  mb_Dp=blocks(a["L1_attn_Dp"])[:, :, 0], mb_A_log=blocks(a["L1_attn_A_log"]),
                  mb_Wx=blocks(a["L1_attn_w_xproj"]), L1_attn_w_dt=a["L1_attn_w_dt"], mb_Wout=blocks(a["L1_attn_w_out"]))
    wide = lambda v: v.transpose(1, 0, 2).reshape(P, -1)
    down = np.concatenate([a["L1_ffn_wd_r"].reshape(-1, P), a["L1_ffn_wd_s"].reshape(-1, P)])
    arrays.update(moe_Wg=wide(a["L1_ffn_wg_r"]), moe_Wu=wide(a["L1_ffn_wu_r"]),
                  moe_Wsh=np.concatenate([wide(a["L1_ffn_wg_s"]), wide(a["L1_ffn_wu_s"]), a["L1_ffn_router_w"]], axis=1),
                  moe_Wd=down.reshape(HB, P, P).transpose(1, 0, 2))
    arrays.update(shape_constants())
    arrays = {"in_" + n: np.ascontiguousarray(v) for n, v in arrays.items()}
    dram = {n[3:]: nc.dram_tensor(n, v.shape, mybir.dt.from_np(v.dtype), kind="ExternalInput").ap()
            for n, v in arrays.items()}
    out = nc.dram_tensor("out_x", (B, T, P), F32, kind="ExternalOutput").ap()
    build(nc, dram, out)
    result = _run(nc, [arrays], core_ids=[0])
    return result.results[0]["out_x"]
```
